# Optimizing a Trainium2 kernel written in Bass

```python
import numpy as np
import jax
import jax.numpy as jnp

def _softmax(x, axis=-1):
    return jax.nn.softmax(x, axis=axis)

def _gelu(x):
    return jax.nn.gelu(x, approximate=True)

def _silu(x):
    return jax.nn.silu(x)

def _sigmoid(x):
    return jax.nn.sigmoid(x)

def _layernorm(x, axis=-1, eps=1e-05):
    m = jnp.mean(x, axis=axis, keepdims=True)
    v = jnp.var(x, axis=axis, keepdims=True)
    return (x - m) / jnp.sqrt(v + eps)

def _scatter_add(tgt, idx, src, axis=0):
    return tgt.at[idx].add(src)

def _segment_sum(src, seg, n):
    return jax.ops.segment_sum(src, seg, n)
kernel_name = 'mk_macaron_d1_jaxref_r8_7f8258'

def setup_inputs(seed: int=0):
    np.random.seed(seed)
    _w = jnp.asarray

    def _L0_attn_setup():
        import jax, jax.numpy as jnp
        import numpy as np
        import math
        D_MODEL = 128
        D_K = 64
        D_V = 64
        N_HEADS = 16
        key = jax.random.key(seed)
        ks = jax.random.split(key, 5)
        std = 1.0 / math.sqrt(D_MODEL)
        x = jax.random.normal(ks[0], (2, 256, D_MODEL), dtype=jnp.float32)
        Wq = jax.random.normal(ks[1], (D_MODEL, N_HEADS * D_K), dtype=jnp.float32) * std
        Wk = jax.random.normal(ks[2], (D_MODEL, N_HEADS * D_K), dtype=jnp.float32) * std
        Wv = jax.random.normal(ks[3], (D_MODEL, N_HEADS * D_V), dtype=jnp.float32) * std
        Wo = jax.random.normal(ks[4], (N_HEADS * D_V, D_MODEL), dtype=jnp.float32) * std
        return {'x': x, 'Wq': Wq, 'Wk': Wk, 'Wv': Wv, 'Wo': Wo}
    _L0_attn_in = _L0_attn_setup()

    def _L0_ffn_setup():
        import jax, jax.numpy as jnp
        import numpy as np
        HIDDEN = 128
        N_EXPERTS = 32
        MOE_I = 64
        N_GROUP = 4
        TOPK_GROUP = 2
        TOP_K = 6
        N_LOCAL_GROUPS = 16
        ANCHOR_I = 32
        SHARED_I = 64
        ROUTED_SCALE = 0.2
        ANCHOR_ALPHA = 0.1
        BATCH, SEQ = (1, 128)

        def _moe_forward(hidden_states, gate_weight, gate_bias, w_gate, w_up, w_down, shared_w_gate, shared_w_up, shared_w_down, anchor_w_gate, anchor_w_up, anchor_w_down):
            B, S, H = hidden_states.shape
            x = hidden_states.reshape(-1, H)
            T = x.shape[0]
            E = gate_weight.shape[0]
            L = anchor_w_gate.shape[0]
            logits = x @ gate_weight.T
            scores = jax.nn.sigmoid(logits)
            sc = scores + gate_bias
            grp = sc.reshape(T, N_GROUP, E // N_GROUP)
            group_scores = jax.lax.top_k(grp, 2)[0].sum(-1)
            _, gidx = jax.lax.top_k(group_scores, TOPK_GROUP)
            gmask = jax.nn.one_hot(gidx, N_GROUP, dtype=sc.dtype).sum(1)
            emask = jnp.repeat(gmask, E // N_GROUP, axis=1)
            masked = jnp.where(emask > 0, sc, -jnp.inf)
            _, topidx = jax.lax.top_k(masked, TOP_K)
            tw = jnp.take_along_axis(scores, topidx, axis=-1)
            tw = tw / (tw.sum(-1, keepdims=True) + 1e-20) * ROUTED_SCALE
            g = jnp.einsum('th,ehi->tei', x, w_gate)
            u = jnp.einsum('th,ehi->tei', x, w_up)
            eo = jnp.einsum('tei,eih->teh', jax.nn.silu(g) * u, w_down)
            cw = (jax.nn.one_hot(topidx, E, dtype=x.dtype) * tw[..., None]).sum(1)
            routed = jnp.einsum('te,teh->th', cw, eo)
            shared = jax.nn.silu(x @ shared_w_gate) * (x @ shared_w_up) @ shared_w_down
            lg = topidx[:, 0] // (E // L)
            ag = jnp.einsum('th,lhi->tli', x, anchor_w_gate)
            au = jnp.einsum('th,lhi->tli', x, anchor_w_up)
            ao = jnp.einsum('tli,lih->tlh', jax.nn.silu(ag) * au, anchor_w_down)
            acw = jax.nn.one_hot(lg, L, dtype=x.dtype)
            anchor = jnp.einsum('tl,tlh->th', acw, ao)
            out = routed + shared + ANCHOR_ALPHA * anchor
            return out.reshape(B, S, H)
        key = jax.random.key(seed)
        ks = jax.random.split(key, 13)
        s = 0.02
        return {'hidden_states': jax.random.normal(ks[0], (BATCH, SEQ, HIDDEN), jnp.float32), 'gate_weight': s * jax.random.normal(ks[1], (N_EXPERTS, HIDDEN), jnp.float32), 'gate_bias': s * jax.random.normal(ks[2], (N_EXPERTS,), jnp.float32), 'w_gate': s * jax.random.normal(ks[3], (N_EXPERTS, HIDDEN, MOE_I), jnp.float32), 'w_up': s * jax.random.normal(ks[4], (N_EXPERTS, HIDDEN, MOE_I), jnp.float32), 'w_down': s * jax.random.normal(ks[5], (N_EXPERTS, MOE_I, HIDDEN), jnp.float32), 'shared_w_gate': s * jax.random.normal(ks[6], (HIDDEN, SHARED_I), jnp.float32), 'shared_w_up': s * jax.random.normal(ks[7], (HIDDEN, SHARED_I), jnp.float32), 'shared_w_down': s * jax.random.normal(ks[8], (SHARED_I, HIDDEN), jnp.float32), 'anchor_w_gate': s * jax.random.normal(ks[9], (N_LOCAL_GROUPS, HIDDEN, ANCHOR_I), jnp.float32), 'anchor_w_up': s * jax.random.normal(ks[10], (N_LOCAL_GROUPS, HIDDEN, ANCHOR_I), jnp.float32), 'anchor_w_down': s * jax.random.normal(ks[11], (N_LOCAL_GROUPS, ANCHOR_I, HIDDEN), jnp.float32)}
    _L0_ffn_in = _L0_ffn_setup()
    _d = {'L0_attn_x': _L0_attn_in['x'], 'L0_attn_Wq': _L0_attn_in['Wq'], 'L0_attn_Wk': _L0_attn_in['Wk'], 'L0_attn_Wv': _L0_attn_in['Wv'], 'L0_attn_Wo': _L0_attn_in['Wo'], 'L0_ffn_gate_weight': _L0_ffn_in['gate_weight'], 'L0_ffn_gate_bias': _L0_ffn_in['gate_bias'], 'L0_ffn_w_gate': _L0_ffn_in['w_gate'], 'L0_ffn_w_up': _L0_ffn_in['w_up'], 'L0_ffn_w_down': _L0_ffn_in['w_down'], 'L0_ffn_shared_w_gate': _L0_ffn_in['shared_w_gate'], 'L0_ffn_shared_w_up': _L0_ffn_in['shared_w_up'], 'L0_ffn_shared_w_down': _L0_ffn_in['shared_w_down'], 'L0_ffn_anchor_w_gate': _L0_ffn_in['anchor_w_gate'], 'L0_ffn_anchor_w_up': _L0_ffn_in['anchor_w_up'], 'L0_ffn_anchor_w_down': _L0_ffn_in['anchor_w_down']}
    _x0 = _d['L0_attn_x']
    _d['L0_attn_x'] = jax.random.normal(jax.random.fold_in(jax.random.key(seed), 1), (8, 512, 128), dtype=_x0.dtype)
    del _x0
    return _d

def reference(L0_attn_x, L0_attn_Wq, L0_attn_Wk, L0_attn_Wv, L0_attn_Wo, L0_ffn_gate_weight, L0_ffn_gate_bias, L0_ffn_w_gate, L0_ffn_w_up, L0_ffn_w_down, L0_ffn_shared_w_gate, L0_ffn_shared_w_up, L0_ffn_shared_w_down, L0_ffn_anchor_w_gate, L0_ffn_anchor_w_up, L0_ffn_anchor_w_down):

    def _L0_attn_ref(x, Wq, Wk, Wv, Wo):
        import jax, jax.numpy as jnp
        import numpy as np
        import math
        D_MODEL = 128
        D_K = 64
        D_V = 64
        N_HEADS = 16
        B, S, D = x.shape
        H, dk, dv = (N_HEADS, D_K, D_V)
        q = (x @ Wq).reshape(B, S, H, dk)
        k = (x @ Wk).reshape(B, S, H, dk)
        v = (x @ Wv).reshape(B, S, H, dv)
        scores = jnp.einsum('bqhd,bkhd->bhqk', q / math.sqrt(dk), k)
        causal = jnp.tril(jnp.ones((S, S), dtype=bool))
        scores = scores + jnp.where(causal, 0.0, -jnp.inf).astype(scores.dtype)
        attn = jax.nn.softmax(scores, axis=-1)
        out = jnp.einsum('bhqk,bkhd->bqhd', attn, v).reshape(B, S, H * dv)
        return x + out @ Wo

    def _L0_ffn_ref(hidden_states, gate_weight, gate_bias, w_gate, w_up, w_down, shared_w_gate, shared_w_up, shared_w_down, anchor_w_gate, anchor_w_up, anchor_w_down):
        import jax, jax.numpy as jnp
        import numpy as np
        HIDDEN = 128
        N_EXPERTS = 32
        MOE_I = 64
        N_GROUP = 4
        TOPK_GROUP = 2
        TOP_K = 6
        N_LOCAL_GROUPS = 16
        ANCHOR_I = 32
        SHARED_I = 64
        ROUTED_SCALE = 0.2
        ANCHOR_ALPHA = 0.1
        BATCH, SEQ = (1, 128)

        def _moe_forward(hidden_states, gate_weight, gate_bias, w_gate, w_up, w_down, shared_w_gate, shared_w_up, shared_w_down, anchor_w_gate, anchor_w_up, anchor_w_down):
            B, S, H = hidden_states.shape
            x = hidden_states.reshape(-1, H)
            T = x.shape[0]
            E = gate_weight.shape[0]
            L = anchor_w_gate.shape[0]
            logits = x @ gate_weight.T
            scores = jax.nn.sigmoid(logits)
            sc = scores + gate_bias
            grp = sc.reshape(T, N_GROUP, E // N_GROUP)
            group_scores = jax.lax.top_k(grp, 2)[0].sum(-1)
            _, gidx = jax.lax.top_k(group_scores, TOPK_GROUP)
            gmask = jax.nn.one_hot(gidx, N_GROUP, dtype=sc.dtype).sum(1)
            emask = jnp.repeat(gmask, E // N_GROUP, axis=1)
            masked = jnp.where(emask > 0, sc, -jnp.inf)
            _, topidx = jax.lax.top_k(masked, TOP_K)
            tw = jnp.take_along_axis(scores, topidx, axis=-1)
            tw = tw / (tw.sum(-1, keepdims=True) + 1e-20) * ROUTED_SCALE
            g = jnp.einsum('th,ehi->tei', x, w_gate)
            u = jnp.einsum('th,ehi->tei', x, w_up)
            eo = jnp.einsum('tei,eih->teh', jax.nn.silu(g) * u, w_down)
            cw = (jax.nn.one_hot(topidx, E, dtype=x.dtype) * tw[..., None]).sum(1)
            routed = jnp.einsum('te,teh->th', cw, eo)
            shared = jax.nn.silu(x @ shared_w_gate) * (x @ shared_w_up) @ shared_w_down
            lg = topidx[:, 0] // (E // L)
            ag = jnp.einsum('th,lhi->tli', x, anchor_w_gate)
            au = jnp.einsum('th,lhi->tli', x, anchor_w_up)
            ao = jnp.einsum('tli,lih->tlh', jax.nn.silu(ag) * au, anchor_w_down)
            acw = jax.nn.one_hot(lg, L, dtype=x.dtype)
            anchor = jnp.einsum('tl,tlh->th', acw, ao)
            out = routed + shared + ANCHOR_ALPHA * anchor
            return out.reshape(B, S, H)
        return _moe_forward(hidden_states, gate_weight, gate_bias, w_gate, w_up, w_down, shared_w_gate, shared_w_up, shared_w_down, anchor_w_gate, anchor_w_up, anchor_w_down)
    x = L0_attn_x
    x = x + 0.5 * _L0_ffn_ref(_layernorm(x, axis=-1), L0_ffn_gate_weight, L0_ffn_gate_bias, L0_ffn_w_gate, L0_ffn_w_up, L0_ffn_w_down, L0_ffn_shared_w_gate, L0_ffn_shared_w_up, L0_ffn_shared_w_down, L0_ffn_anchor_w_gate, L0_ffn_anchor_w_up, L0_ffn_anchor_w_down)
    x = x + _L0_attn_ref(_layernorm(x, axis=-1), L0_attn_Wq, L0_attn_Wk, L0_attn_Wv, L0_attn_Wo)
    x = x + 0.5 * _L0_ffn_ref(_layernorm(x, axis=-1), L0_ffn_gate_weight, L0_ffn_gate_bias, L0_ffn_w_gate, L0_ffn_w_up, L0_ffn_w_down, L0_ffn_shared_w_gate, L0_ffn_shared_w_up, L0_ffn_shared_w_down, L0_ffn_anchor_w_gate, L0_ffn_anchor_w_up, L0_ffn_anchor_w_down)
    return x

_drawn_inputs = setup_inputs


def setup_inputs(seed=0):
    import zlib

    import numpy as np

    out = dict(_drawn_inputs(seed))
    spreads = {}
    factors = {'L0_ffn_gate_weight': 8.0,
     'L0_ffn_gate_bias': 8.0,
     'L0_ffn_w_gate': 8.0,
     'L0_ffn_w_up': 8.0,
     'L0_ffn_w_down': 8.0,
     'L0_ffn_shared_w_gate': 8.0,
     'L0_ffn_shared_w_up': 8.0,
     'L0_ffn_shared_w_down': 8.0,
     'L0_ffn_anchor_w_gate': 8.0,
     'L0_ffn_anchor_w_up': 8.0,
     'L0_ffn_anchor_w_down': 8.0}
    for name, (base, spread) in spreads.items():
        noise = np.random.default_rng([zlib.crc32(name.encode()), seed]).standard_normal(out[name].shape)
        drawn = base * np.exp(spread * noise) if base else spread * noise
        out[name] = jnp.asarray(drawn.astype(out[name].dtype))
    for name, factor in factors.items():
        out[name] = (out[name] * factor).astype(out[name].dtype)
    return out
```

```python
from contextlib import ExitStack

import numpy as np

import concourse.bass as bass
from concourse import mybir

ALU = mybir.AluOpType
ACT = mybir.ActivationFunctionType
AX = mybir.AxisListType
F32 = mybir.dt.float32
F32R = mybir.dt.float32r
BF16 = mybir.dt.bfloat16
U32 = mybir.dt.uint32

P = 128
TB = 4
CH = TB * P
E, G, TOPK, MI = 32, 4, 6, 64
EG = E // G
L, AI = 16, 32
ROWS = 64
HT = (E * MI + L * AI + MI + P - 1) // P
H, DK = 16, 64
LAG = 3
NEG = -1.0e30
EPS = 1e-5
KB_OFF = [0, 640 + 128, 1152, 640]
PT_W = 1408
PW = TB * (TB + 1) // 2 * P
CONV_GROUPS = 3
GT = HT // CONV_GROUPS


def constants():
    ident = np.eye(P, dtype=np.float32)
    sel = np.zeros((P, HT, P), np.float32)
    for row in range(HT * P):
        if row < E * MI:
            src = row // MI
        elif row < E * MI + L * AI:
            src = E + (row - E * MI) // AI
        else:
            src = E + L
        sel[src, row // P, row % P] = 1.0
        sel[ROWS + src, row // P, row % P] = 1.0
    mask = np.where(np.arange(P)[None, :] > np.arange(P)[:, None], NEG, 0.0)
    iota = np.broadcast_to(np.arange(E, dtype=np.float32)[None, :, None], (P, E, TOPK))
    tie = np.broadcast_to((np.arange(G)[None, :] < np.arange(G)[:, None]), (P, TB, G, G))
    small = np.concatenate([ident, mask, iota.reshape(P, -1), tie.reshape(P, -1)], 1)
    return small.astype(np.float32), sel.reshape(P, -1)


def build(nc, x_in, wg_in, wu_in, wd_in, gate_in, bias_in, wqT_in, wkT_in, wvT_in, wo_in,
          small_in, sel_in, out):
    T = x_in.shape[0]
    NT = T // P
    NC = T // CH
    HC = HT * P
    ctx = ExitStack()
    with ctx:
        def sb(name, shape, dt=F32):
            return ctx.enter_context(nc.sbuf_tensor(name, shape, dt))

        def sem(name):
            return ctx.enter_context(nc.semaphore(name))

        small = sb("small", [P, 2 * P + E * TOPK + TB * G * G])
        ident = small[:, 0:P]
        iota = small[:, 2 * P:2 * P + E * TOPK].rearrange("p (e k) -> p e k", e=E)
        tie = small[:, 2 * P + E * TOPK:].rearrange("p (t a b) -> p t a b", t=TB, a=G)
        half = sb("half", [P, 2 * P], BF16)
        ident_bf, mask_bf = half[:, 0:P], half[:, P:2 * P]
        sel = sb("sel", [P, HC], F32R)
        gate_w = sb("gate_w", [P, E])
        bias = sb("bias", [P, E])
        wg = [sb(f"wg_{n}", [P, HC], F32R) for n in ("hi", "lo")]
        wu = [sb(f"wu_{n}", [P, HC], F32R) for n in ("hi", "lo")]
        wd = [sb(f"wd_{n}", [P, HC], F32R) for n in ("hi", "lo")]
        stage = sb("stage", [P, 2, 3, GT * P])
        attn_w = stage[:, :, :, :].rearrange("p a b c -> p (a b c)")[:, 0:4 * H * DK] \
            .rearrange("p (w j d) -> p w j d", w=4, j=H // 2)
        mh = [sb(f"m_{n}", [P, H * P], F32R) for n in ("hi", "lo")]
        bh = sb("b_h", [P, H * P])
        x = sb("x", [P, NT, P])
        bn = sb("bn", [P, TB, 6])
        mean_var = sb("mean_var", [P, TB, 2])
        mean = sb("mean", [P, NT])
        var_eps = sb("var_eps", [P, NT])
        std = sb("std", [P, NT])
        rstd0 = sb("rstd0", [P, NT])
        newton = sb("newton", [P, NT])
        pace = sb("pace", [P, 1])
        rstd = sb("rstd", [P, NT])
        xn = sb("xn", [P, TB, P])
        xT = sb("xT", [P, CH])
        xTp = [sb(f"xT_{n}", [P, CH], F32R) for n in ("hi", "lo")]
        score = sb("score", [P, TB, E])
        sc = sb("sc", [P, TB, E])
        t4 = [sb(f"t4_{i}", [P, TB * G, 4]) for i in range(2)]
        t2 = [sb(f"t2_{i}", [P, TB * G, 2]) for i in range(4)]
        t1 = [sb(f"t1_{i}", [P, TB * G, 1]) for i in range(4)]
        gscore = sb("gscore", [P, TB * G, 1])
        gcmp = [sb(f"gcmp_{i}", [P, TB, G, G]) for i in range(3)]
        grank = sb("grank", [P, TB * G, 1])
        gpen = sb("gpen", [P, TB * G, 1])
        masked = sb("masked", [P, TB, E])
        top = sb("top", [P, TB, 8])
        topi = sb("topi", [P, TB, 8], U32)
        topf = sb("topf", [P, TB, 8])
        onehot = sb("onehot", [P, TB, E, TOPK])
        chosen = sb("chosen", [P, TB, E])
        wts = sb("wts", [P, TB, E])
        wsum = sb("wsum", [P, TB, 1])
        wsum_e = sb("wsum_e", [P, TB, 1])
        wrec = sb("wrec", [P, TB, 1])
        wfac = sb("wfac", [P, TB, 1])
        anch = sb("anch", [P, TB, L])
        cw = sb("cw", [P, TB, ROWS])
        cw2 = sb("cw2", [P, TB, 2 * ROWS])
        cwT = sb("cwT", [P, CH], F32R)
        prob = sb("prob", [P, 2, PW])
        pT = [sb(f"pT_{n}", [P, 2, PT_W], F32R) for n in ("hi", "lo")]
        yh = [sb(f"y_{n}", [P, 2, CH], F32R) for n in ("hi", "lo")]
        xnp = [sb(f"xn_{n}", [P, TB, P], F32R) for n in ("hi", "lo")]
        ctxT = sb("ctxT", [P, 2, CH])
        yT = ctxT[:, 0, :]
        nmax = sb("nmax", [P, 2, TB])
        rsum = sb("rsum", [P, 2, TB])
        rrec = sb("rrec", [P, 2, TB])
        ffn_f = prob[:, :, :].rearrange("p a b -> p (a b)")
        silu = [ffn_f[:, i * CH:(i + 1) * CH] for i in (0, 1)]
        z = [ffn_f[:, i * CH:(i + 1) * CH] for i in (2, 3, 4)]
        NZ = 5
        pT_flat = [t[:, :, :].rearrange("p a b -> p (a b)") for t in pT]
        zp = [[t[:, i * CH:(i + 1) * CH] for i in range(NZ)] for t in pT_flat]

        bank = [ctx.enter_context(nc.psum_tensor(f"bank{i}", [P, 512], F32)) for i in range(8)]
        psG, psU, psW, psY, psM = bank[0:2], bank[2:4], bank[4:6], bank[6], bank[7]
        psS, psPT, psYh, psC, psO = bank[0:2], bank[2:5], bank[5], bank[6], bank[7]

        names = """consts_loaded sel_loaded attn_w_loaded
            wsplit_hi wsplit_lo stat_dve stat_act stat_rows stat_bn cw_const
            xn_ready xT_ps xT_sb logits_ps sigmoid_done route cwT_ps cwT_sb xT_hi xT_lo
            gate_up_ps spread_ps silu_done gated_done z_done z_hi z_lo down_ps
            y_evac yT_ps x_added
            mb_ps mb_hi mb_lo zeroed
            a_xn a_xT_ps a_xT_sb a_xT_hi a_xT_lo a_xres a_xn_hi a_xn_lo
            yh_ps yh_hi yh_lo s_ps max_done exp_done rec_done norm_done
            pT_ps pT_hi pT_lo ctx_ps ctx_sb out_ps out_added stored""".split()
        s = {n: sem("s_" + n) for n in names}
        x_loads = [sem(f"s_x_load{c}") for c in range(NC)]
        w_loads = [sem(f"s_w_load{k}") for k in range(CONV_GROUPS)]

        block = ctx.enter_context(nc.Block())

        def f32(ap):
            return ap.bitcast(F32)

        def mm3(pe, o, w, m, start, stop):
            pe.matmul(o, w[0], m[0], start=start, stop=False, skip_group_check=True)
            pe.matmul(o, w[0], m[1], start=False, stop=False, skip_group_check=True)
            return pe.matmul(o, w[1], m[0], start=False, stop=stop, skip_group_check=True)

        def tiles(g, j):
            return g * HT + j + 1

        def two_ago(g, j):
            return g * HT + (j - 1 if j > 1 else -j)

        def part_slot(j):
            return j % 4 if j < HT - 1 else 4

        def part_slot_free(g, j):
            return tiles(g, j) - (HT if j == HT - 1 else 4 if j > 3 else 5)

        ROUTE = 40

        def weight_heads(k):
            k %= H // TB
            return [(k // 2) * 2 * TB + 2 * i + k % 2 for i in range(TB)]

        def head_columns(t, k):
            h = weight_heads(k)[0]
            return t[:, :].rearrange("p (j two d) -> p j two d", two=2, d=P)[:, h // 2:h // 2 + TB, h % 2, :]

        @block.sync
        def _(sp):
            def load_group(sp, k):
                cols = slice(k * GT * P, (k + 1) * GT * P)
                for w, src in enumerate((wg_in, wu_in, wd_in)):
                    sp.dma_start(stage[:, k % 2, w, :], src[:, cols]).then_inc(w_loads[k], 16)

            sp.dma_start(small[:, :], small_in).then_inc(s["consts_loaded"], 16)
            sp.dma_start(gate_w[:, :], gate_in).then_inc(s["consts_loaded"], 16)
            sp.dma_start(bias[:, :], bias_in.partition_broadcast(P)).then_inc(s["consts_loaded"], 16)
            for c in range(NC):
                sp.dma_start(x[:, c * TB:(c + 1) * TB, :],
                             x_in[c * CH:(c + 1) * CH, :].rearrange("(t p) d -> p t d", p=P)) \
                    .then_inc(x_loads[c], 16)
                if c < 2:
                    load_group(sp, c)
            for k in range(2, CONV_GROUPS):
                sp.wait_ge(s["wsplit_lo"], 3 * (k - 1))
                load_group(sp, k)
            sp.wait_ge(s["wsplit_lo"], 3 * CONV_GROUPS)
            for w, src in enumerate((wqT_in, wkT_in, wvT_in, wo_in)):
                sp.dma_start(attn_w[:, w, :, :], src.rearrange("(j p) d -> p j d", p=P)) \
                    .then_inc(s["attn_w_loaded"], 16)
            with sp.Fori(0, NC) as c:
                sp.wait_ge(s["x_added"], (c + NC) + 1)
                sp.dma_start(out[bass.ds(c * CH, CH), :].rearrange("(t p) d -> p t d", p=P),
                             x[:, bass.ds(c * TB, TB), :]).then_inc(s["stored"], 16)
            sp.wait_ge(s["stored"], 16 * NC)

        @block.tensor
        def _(pe):
            def to_columns(dst, src, n=TB):
                for t in range(n):
                    m = pe.transpose(dst[:, t * P:(t + 1) * P], src[:, t, :], ident)
                return m

            def prep_xT(g):
                pe.wait_ge(s["xn_ready"], g + 1)
                to_columns(psM, xn).then_inc(s["xT_ps"], 1)

            def prep_logits(g):
                pe.wait_ge(s["xT_sb"], g + 1)
                for t in range(TB):
                    m = pe.matmul(psM[:, t * E:(t + 1) * E], xT[:, t * P:(t + 1) * P], gate_w[:, :],
                                  start=True, stop=True, skip_group_check=True)
                m.then_inc(s["logits_ps"], 1)

            def prep_cwT(g):
                pe.wait_ge(s["route"], (g + 1) * ROUTE)
                to_columns(psM, cw2).then_inc(s["cwT_ps"], 1)

            def gate_up(g, j, first):
                if j == 0:
                    pe.wait_ge(s["xT_hi"], g + 1)
                    pe.wait_ge(s["xT_lo"], g + 1)
                if not (first and j < 2):
                    pe.wait_ge(s["silu_done"], two_ago(g, j))
                    pe.wait_ge(s["gated_done"], two_ago(g, j))
                c = slice(j * P, (j + 1) * P)
                mm3(pe, psG[j % 2][:, :], [w[:, c] for w in wg], [t[:, :] for t in xTp], True, True)
                mm3(pe, psU[j % 2][:, :], [w[:, c] for w in wu], [t[:, :] for t in xTp], True, True) \
                    .then_inc(s["gate_up_ps"], 1)

            def spread(g, j, first):
                if j == 0:
                    pe.wait_ge(s["cwT_sb"], g + 1)
                if not (first and j < 2):
                    pe.wait_ge(s["z_done"], two_ago(g, j))
                pe.matmul(psW[j % 2][:, :], sel[:, j * P:(j + 1) * P], cwT[:, :],
                          start=True, stop=True).then_inc(s["spread_ps"], 1)

            def down(g, j, first):
                pe.wait_ge(s["z_hi"], tiles(g, j))
                pe.wait_ge(s["z_lo"], tiles(g, j))
                if j == 0 and not first:
                    pe.wait_ge(s["y_evac"], g)
                c = slice(j * P, (j + 1) * P)
                mm3(pe, psY[:, :], [w[:, c] for w in wd], [zp[0][part_slot(j)], zp[1][part_slot(j)]],
                    j == 0, j == HT - 1).then_inc(s["down_ps"], 1)

            def post_yT(g):
                pe.wait_ge(s["y_evac"], g + 1)
                to_columns(psM, yT.rearrange("p (t d) -> p t d", t=TB)).then_inc(s["yT_ps"], 1)

            def ffn_chunk(g, first, last, setup=False):
                for j in range(HT):
                    if setup and j % GT == 0:
                        pe.wait_ge(s["wsplit_lo"], 3 * (j // GT + 1))
                        pe.wait_ge(s["wsplit_hi"], 3 * (j // GT + 1))
                    if j == 2 and not last:
                        prep_xT(g + 1)
                    if j == 4 and not last:
                        prep_logits(g + 1)
                    if j == 7 and not first:
                        if not last:
                            pe.wait_ge(s["sigmoid_done"], g + 2)
                        post_yT(g - 1)
                    if j == HT - 1 and not last:
                        if not first:
                            pe.wait_ge(s["x_added"], g)
                        else:
                            pe.wait_ge(s["sigmoid_done"], g + 2)
                        prep_cwT(g + 1)
                    gate_up(g, j, first)
                    spread(g, j, first)
                    if j >= LAG:
                        down(g, j - LAG, first)
                    elif not first:
                        down(g - 1, HT - LAG + j, False)

            def ffn(g0):
                prep_xT(g0)
                prep_logits(g0)
                pe.wait_ge(s["sigmoid_done"], g0 + 1)
                prep_cwT(g0)
                if g0 == 0:
                    pe.wait_ge(s["sel_loaded"], 16)
                ffn_chunk(g0, True, False, setup=g0 == 0)
                with pe.Fori(g0 + 1, g0 + NC - 1) as g:
                    ffn_chunk(g, False, False)
                ffn_chunk(g0 + NC - 1, False, True)
                for j in range(HT - LAG, HT):
                    down(g0 + NC - 1, j, False)
                pe.wait_ge(s["x_added"], g0 + NC - 1)
                post_yT(g0 + NC - 1)

            def a_prep(b):
                pe.wait_ge(s["a_xn"], b + 1)
                to_columns(psYh, xn).then_inc(s["a_xT_ps"], 1)

            def head_y(b, h):
                n = b * H + h
                if h == 0:
                    pe.wait_ge(s["a_xT_hi"], b + 1)
                    pe.wait_ge(s["a_xT_lo"], b + 1)
                else:
                    pe.wait_ge(s["yh_lo"], n)
                c = slice(h * P, (h + 1) * P)
                mm3(pe, psYh[:, :], [w[:, c] for w in mh], [t[:, :] for t in xTp], True, True) \
                    .then_inc(s["yh_ps"], 1)

            def head_scores(b, h, qb, first):
                n = b * H + h
                pe.wait_ge(s["yh_hi"], n + 1)
                pe.wait_ge(s["yh_lo"], n + 1)
                if not (first and h == 0 and qb > 1):
                    pe.wait_ge(s["exp_done"], n * TB + (TB - 1 - qb) - 1)
                w = max(2, qb + 1) * P
                ps = psS[qb % 2]
                q = slice(qb * P, (qb + 1) * P)
                mm3(pe, ps[:, 0:w], [t[:, h % 2, q] for t in yh], [t[:, 0:w] for t in xTp], True, False)
                pe.matmul(ps[:, q], ident_bf, mask_bf, start=False, stop=True,
                          skip_group_check=True).then_inc(s["s_ps"], 1)

            def head_probT(b, h, part, first):
                n = b * H + h
                pe.wait_ge(s["norm_done"], n * TB + TB)
                if not (first and h == 0):
                    pe.wait_ge(s["pT_hi"], (n - 1) * 3 + part + 1)
                    pe.wait_ge(s["pT_lo"], (n - 1) * 3 + part + 1)
                blocks = [[(0, q) for q in range(TB)],
                          [(3, 3)] + [(1, q) for q in range(1, TB)],
                          [(2, q) for q in range(2, TB)]][part]
                for i, (kb, q) in enumerate(blocks):
                    o = q * (q + 1) // 2 * P + kb * P
                    m = pe.transpose(psPT[part][:, i * P:(i + 1) * P], prob[:, h % 2, o:o + P], ident)
                m.then_inc(s["pT_ps"], 1)

            def head_pv(b, h, kb, first):
                n = b * H + h
                if kb == 0:
                    pe.wait_ge(s["pT_hi"], n * 3 + 1)
                    pe.wait_ge(s["pT_lo"], n * 3 + 1)
                    if h == 0:
                        pe.wait_ge(s["a_xn_hi"], b + 1)
                        pe.wait_ge(s["a_xn_lo"], b + 1)
                    if not (first and h == 0):
                        pe.wait_ge(s["ctx_sb"], n)
                else:
                    pe.wait_ge(s["pT_hi"], n * 3 + (2 if kb == 1 else 3))
                    pe.wait_ge(s["pT_lo"], n * 3 + (2 if kb == 1 else 3))
                q0 = min(kb, TB - 2) * P
                o = KB_OFF[kb] - (P if kb == 3 else 0)
                w = CH - q0
                m = mm3(pe, psC[:, q0:CH], [t[:, kb, :] for t in xnp],
                        [t[:, h % 2, o:o + w] for t in pT], kb == 0, kb == 3)
                if kb == 3:
                    m.then_inc(s["ctx_ps"], 1)

            def head_out(b, h, first):
                n = b * H + h
                pe.wait_ge(s["ctx_sb"], n + 1)
                if h == 0 and not first:
                    pe.wait_ge(s["out_added"], b)
                for t in range(TB):
                    m = pe.matmul(psO[:, t * P:(t + 1) * P], ctxT[:, h % 2, t * P:(t + 1) * P],
                                  bh[:, h * P:(h + 1) * P], start=(h == 0 and t == 0),
                                  stop=(h == H - 1 and t == TB - 1), skip_group_check=True)
                m.then_inc(s["out_ps"], 1)

            def attn_slot(b, sl, first, last):
                nxt = lambda k: (b, sl + k) if sl + k < H else (b + 1, sl + k - H)
                prv = lambda k: (b, sl - k) if sl >= k else (b - 1, sl - k + H)
                have_y = not (last and sl + 2 >= H)
                have_s = not (last and sl + 1 >= H)
                have_v = not (first and sl < 1)
                have_o = not (first and sl < 2)
                if have_s:
                    head_scores(*nxt(1), 3, False)
                if sl == 11 and not last:
                    pe.wait_ge(s["a_xT_sb"], b + 2)
                if have_y and sl + 2 != H:
                    head_y(*nxt(2))
                if have_v:
                    head_pv(*prv(1), 0, first and sl < 2)
                if sl == 10 and not last:
                    pe.wait_ge(s["yh_lo"], b * H + 13)
                    a_prep(b + 1)
                head_probT(b, sl, 0, first)
                if have_s:
                    head_scores(*nxt(1), 2, False)
                head_probT(b, sl, 1, first)
                if have_v:
                    head_pv(*prv(1), 1, first)
                if have_s:
                    head_scores(*nxt(1), 1, False)
                head_probT(b, sl, 2, first)
                if have_s:
                    head_scores(*nxt(1), 0, False)
                if have_v:
                    head_pv(*prv(1), 2, first)
                    head_pv(*prv(1), 3, first)
                if have_o:
                    head_out(*prv(2), first and sl - 2 < H)
                if have_y and sl + 2 == H:
                    head_y(*nxt(2))

            def attention():
                pe.wait_ge(s["attn_w_loaded"], 64)
                for k in range(2 * H // TB):
                    if k == 0:
                        pe.wait_ge(s["gated_done"], NC * HT)
                    if k > 1:
                        pe.wait_ge(s["mb_hi"], k - 1)
                        pe.wait_ge(s["mb_lo"], min(k - 1, H // TB))
                    for i in range(TB):
                        h = weight_heads(k)[i]
                        r = slice((h % 2) * DK, (h % 2) * DK + DK)
                        a, c = (0, 1) if k < H // TB else (2, 3)
                        m = pe.matmul(psG[k % 2][:, i * P:(i + 1) * P], attn_w[r, a, h // 2, :],
                                      attn_w[r, c, h // 2, :], start=True, stop=True,
                                      skip_group_check=True)
                    m.then_inc(s["mb_ps"], 1)
                pe.wait_ge(s["x_added"], NC)
                a_prep(0)
                pe.wait_ge(s["zeroed"], 1)
                pe.wait_ge(s["cw_const"], 1)
                pe.wait_ge(s["mb_hi"], 2 * H // TB)
                pe.wait_ge(s["mb_lo"], H // TB)
                head_y(0, 0)
                for qb in (3, 2, 1, 0):
                    head_scores(0, 0, qb, True)
                head_y(0, 1)
                for sl in range(H):
                    attn_slot(0, sl, True, False)
                with pe.Fori(1, NC - 1) as b:
                    for sl in range(H):
                        attn_slot(b, sl, False, False)
                for sl in range(H):
                    attn_slot(NC - 1, sl, False, True)
                for kb in range(TB):
                    head_pv(NC - 1, H - 1, kb, False)
                head_out(NC - 1, H - 2, False)
                head_out(NC - 1, H - 1, False)
                pe.wait_ge(s["out_added"], NC)

            ffn(0)
            attention()
            ffn(NC)

        @block.scalar
        def _(act):
            def row_std(n):
                act.wait_ge(s["stat_bn"], n * NC)
                nc.scalar.activation(std[:, :], var_eps[:, :], ACT.Sqrt).then_inc(s["stat_act"], 1)

            def prep_copy(g):
                act.wait_ge(s["xT_ps"], g + 1)
                nc.scalar.activation(xT[:, :], psM[:, :], ACT.Copy).then_inc(s["xT_sb"], 1)

            def prep_sigmoid(g, first=False):
                act.wait_ge(s["logits_ps"], g + 1)
                if not first:
                    act.wait_ge(s["route"], g * ROUTE)
                nc.scalar.activation(score[:, :, :].rearrange("p t e -> p (t e)"), psM[:, 0:TB * E],
                                     ACT.Sigmoid).then_inc(s["sigmoid_done"], 1)

            def prep_parts(g, first):
                if not first:
                    act.wait_ge(s["gate_up_ps"], g * HT)
                else:
                    act.wait_ge(s["xT_sb"], g + 1)
                nc.scalar.activation(xTp[0][:, :], xT[:, :], ACT.Copy).then_inc(s["xT_hi"], 1)
                if not first:
                    act.wait_ge(s["spread_ps"], g * HT)
                act.wait_ge(s["cwT_ps"], g + 1)
                nc.scalar.activation(cwT[:, :], psM[:, :], ACT.Copy).then_inc(s["cwT_sb"], 1)

            def z_hi(g, j, early):
                act.wait_ge(s["z_done"], tiles(g, j))
                if not early:
                    act.wait_ge(s["down_ps"], part_slot_free(g, j))
                nc.scalar.activation(zp[0][part_slot(j)], z[j % 3], ACT.Copy).then_inc(s["z_hi"], 1)

            def y_copy(g):
                act.wait_ge(s["down_ps"], tiles(g, HT - 1))
                nc.scalar.activation(yT, psY[:, :], ACT.Copy).then_inc(s["y_evac"], 1)

            def split_group_hi(k):
                act.wait_ge(w_loads[k], 48)
                c = slice(k * GT * P, (k + 1) * GT * P)
                for w, dst in enumerate((wg, wu, wd)):
                    nc.scalar.activation(dst[0][:, c], stage[:, k % 2, w, :], ACT.Copy) \
                        .then_inc(s["wsplit_hi"], 1)

            def ffn_chunk(g, first, last, setup=False):
                for j in range(HT):
                    if j == 3 and not last:
                        prep_copy(g + 1)
                    if j == 3 and not first:
                        y_copy(g - 1)
                    if j == 5 and not last:
                        prep_sigmoid(g + 1)
                    act.wait_ge(s["gate_up_ps"], tiles(g, j))
                    if not (first and j < 2):
                        act.wait_ge(s["gated_done"], two_ago(g, j))
                    nc.scalar.activation(silu[j % 2], psG[j % 2][:, :], ACT.Silu) \
                        .then_inc(s["silu_done"], 1)
                    if j > 0:
                        z_hi(g, j - 1, first and (j - 1 < 4 or j == HT))
                    elif not first:
                        z_hi(g - 1, HT - 1, False)
                if not last:
                    prep_parts(g + 1, False)

            def ffn(g0):
                prep_copy(g0)
                prep_sigmoid(g0, g0 == 0)
                prep_parts(g0, True)
                ffn_chunk(g0, True, False)
                with act.Fori(g0 + 1, g0 + NC - 1) as g:
                    ffn_chunk(g, False, False)
                ffn_chunk(g0 + NC - 1, False, True)
                z_hi(g0 + NC - 1, HT - 1, False)
                y_copy(g0 + NC - 1)

            def a_copy(b):
                act.wait_ge(s["a_xT_ps"], b + 1)
                nc.scalar.activation(xT[:, :], psYh[:, :], ACT.Copy).then_inc(s["a_xT_sb"], 1)

            def a_parts(b, first):
                if not first:
                    act.wait_ge(s["s_ps"], b * H * TB)
                    act.wait_ge(s["yh_ps"], b * H)
                else:
                    act.wait_ge(s["a_xT_sb"], b + 1)
                nc.scalar.activation(xTp[0][:, :], xT[:, :], ACT.Copy).then_inc(s["a_xT_hi"], 1)

            def y_hi(b, h, early):
                n = b * H + h
                act.wait_ge(s["yh_ps"], n + 1)
                if not early:
                    act.wait_ge(s["s_ps"], (n - 1) * TB)
                nc.scalar.activation(yh[0][:, h % 2, :], psYh[:, :], ACT.Copy).then_inc(s["yh_hi"], 1)

            def exp(b, h, qb, early):
                n = b * H + h
                act.wait_ge(s["max_done"], n * TB + TB - qb)
                if not early:
                    act.wait_ge(s["pT_ps"], (n - 1) * 3)
                o = qb * (qb + 1) // 2 * P
                w = (qb + 1) * P
                nc.scalar.activation(prob[:, h % 2, o:o + w], psS[qb % 2][:, 0:w], ACT.Exp,
                                     bias=nmax[:, h % 2, qb:qb + 1],
                                     accum_out=rsum[:, h % 2, qb:qb + 1]).then_inc(s["exp_done"], 1)

            def pT_hi(b, h, part, early):
                n = b * H + h
                act.wait_ge(s["pT_ps"], n * 3 + part + 1)
                if not early:
                    act.wait_ge(s["ctx_ps"], n - 1)
                o, w = ((0, 512), (640, 512), (1152, 256))[part]
                nc.scalar.activation(pT[0][:, h % 2, o:o + w], psPT[part][:, 0:w], ACT.Copy) \
                    .then_inc(s["pT_hi"], 1)

            def ctx_copy(b, h, early):
                n = b * H + h
                act.wait_ge(s["ctx_ps"], n + 1)
                if not early:
                    act.wait_ge(s["out_ps"], n - 1)
                nc.scalar.activation(ctxT[:, h % 2, :], psC[:, :], ACT.Copy).then_inc(s["ctx_sb"], 1)

            def attn_slot(b, sl, first, last):
                nxt = lambda k: (b, sl + k) if sl + k < H else (b + 1, sl + k - H)
                prv = lambda k: (b, sl - k) if sl >= k else (b - 1, sl - k + H)
                have_y = not (last and sl + 2 >= H)
                have_s = not (last and sl + 1 >= H)
                early = first and sl < 1
                if have_s:
                    exp(*nxt(1), 3, early)
                if have_y and sl + 2 != H:
                    y_hi(*nxt(2), False)
                if sl == 10 and not last:
                    a_copy(b + 1)
                pT_hi(b, sl, 0, first and sl < 2)
                if have_s:
                    exp(*nxt(1), 2, early)
                pT_hi(b, sl, 1, first and sl < 2)
                if have_s:
                    exp(*nxt(1), 1, early)
                    exp(*nxt(1), 0, early)
                pT_hi(b, sl, 2, first and sl < 2)
                if have_y and sl + 2 == H:
                    a_parts(b + 1, False)
                if not (first and sl < 1):
                    ctx_copy(*prv(1), first and sl < 3)
                if have_y and sl + 2 == H:
                    y_hi(*nxt(2), False)

            def attention():
                for k in range(2 * H // TB):
                    act.wait_ge(s["mb_ps"], k + 1)
                    src = psG[k % 2][:, :].rearrange("p (j d) -> p j d", d=P)
                    if k < H // TB:
                        nc.scalar.activation(head_columns(mh[0], k), src, ACT.Copy,
                                             scale=float(DK) ** -0.5).then_inc(s["mb_hi"], 1)
                    else:
                        nc.scalar.activation(head_columns(bh, k), src, ACT.Copy) \
                            .then_inc(s["mb_hi"], 1)
                row_std(2)
                a_copy(0)
                a_parts(0, True)
                y_hi(0, 0, True)
                for qb in (3, 2, 1, 0):
                    exp(0, 0, qb, True)
                y_hi(0, 1, True)
                for sl in range(H):
                    attn_slot(0, sl, True, False)
                with act.Fori(1, NC - 1) as b:
                    for sl in range(H):
                        attn_slot(b, sl, False, False)
                for sl in range(H):
                    attn_slot(NC - 1, sl, False, True)
                ctx_copy(NC - 1, H - 1, False)

            row_std(1)
            split_group_hi(0)
            for k in range(1, CONV_GROUPS):
                split_group_hi(k)
            ffn(0)
            attention()
            row_std(3)
            ffn(NC)

        @block.vector
        def _(dve):
            def finish_std(n):
                k = (n - 1) * 5
                dve.wait_ge(s["stat_act"], n)
                nc.vector.reciprocal(rstd0[:, :], std[:, :]).then_inc(s["stat_dve"], 1)
                dve.wait_ge(s["stat_dve"], k + 1)
                nc.vector.tensor_tensor(newton[:, :], rstd0[:, :], rstd0[:, :], ALU.mult) \
                    .then_inc(s["stat_dve"], 1)
                dve.wait_ge(s["stat_dve"], k + 2)
                nc.vector.tensor_tensor(newton[:, :], newton[:, :], var_eps[:, :], ALU.mult) \
                    .then_inc(s["stat_dve"], 1)
                dve.wait_ge(s["stat_dve"], k + 3)
                nc.vector.tensor_scalar(newton[:, :], newton[:, :], -0.5, 1.5, ALU.mult, ALU.add) \
                    .then_inc(s["stat_dve"], 1)
                dve.wait_ge(s["stat_dve"], k + 4)
                nc.vector.tensor_tensor(rstd[:, :], rstd0[:, :], newton[:, :], ALU.mult) \
                    .then_inc(s["stat_dve"], 1)
                dve.wait_ge(s["stat_dve"], k + 5)

            def chunk_stats(c, k):
                nc.vector.tensor_copy(pace[:, :], ident[:, 0:1])
                for t in range(TB):
                    m = nc.vector.bn_stats(bn[:, t, :], x[:, bass.ds(c * TB + t, 1), :]
                                           .rearrange("p a d -> p (a d)"))
                m.then_inc(s["stat_rows"], 1)
                dve.wait_ge(s["stat_rows"], k * 2 + 1)
                nc.vector.tensor_copy(pace[:, :], ident[:, 0:1])
                for t in range(TB):
                    m = nc.vector.bn_aggr(mean_var[:, t, :], bn[:, t, :])
                m.then_inc(s["stat_rows"], 1)
                dve.wait_ge(s["stat_rows"], k * 2 + 2)
                nc.vector.tensor_copy(mean[:, bass.ds(c * TB, TB)], mean_var[:, :, 0])
                nc.vector.tensor_scalar(var_eps[:, bass.ds(c * TB, TB)], mean_var[:, :, 1],
                                        EPS, None, ALU.add).then_inc(s["stat_bn"], 1)

            def normalise(c, done):
                for t in range(TB):
                    m = nc.vector.tensor_scalar(
                        xn[:, t, :], x[:, bass.ds(c * TB + t, 1), :].rearrange("p a d -> p (a d)"),
                        mean[:, bass.ds(c * TB + t, 1)], rstd[:, bass.ds(c * TB + t, 1)],
                        ALU.subtract, ALU.mult)
                m.then_inc(s[done], 1)

            def split_group_lo(k):
                c = slice(k * GT * P, (k + 1) * GT * P)
                for w, dst in enumerate((wg, wu, wd)):
                    dve.wait_ge(s["wsplit_hi"], k * 3 + w + 1)
                    nc.vector.tensor_tensor(dst[1][:, c], stage[:, k % 2, w, :], f32(dst[0][:, c]),
                                            ALU.subtract).then_inc(s["wsplit_lo"], 1)

            def step(ins):
                ins.then_inc(s["route"], 1)

            tt = nc.vector.tensor_tensor

            def route_scores(g):
                dve.wait_ge(s["sigmoid_done"], g + 1)
                step(tt(sc[:, :, :], score[:, :, :], bias[:, :].unsqueeze(1).broadcast_to([P, TB, E]),
                        ALU.add))
                dve.wait_ge(s["route"], g * ROUTE + 1)
                v = sc[:, :, :].rearrange("p t (a b) -> p (t a) b", a=G)
                step(tt(t4[0][:, :, :], v[:, :, 0:4], v[:, :, 4:8], ALU.max))
                step(tt(t4[1][:, :, :], v[:, :, 0:4], v[:, :, 4:8], ALU.min))

            def route_top2(g):
                hi, lo = t4
                dve.wait_ge(s["route"], g * ROUTE + 3)
                step(tt(t2[0][:, :, :], hi[:, :, 0:2], hi[:, :, 2:4], ALU.max))
                step(tt(t2[1][:, :, :], hi[:, :, 0:2], hi[:, :, 2:4], ALU.min))
                step(tt(t2[2][:, :, :], lo[:, :, 0:2], lo[:, :, 2:4], ALU.max))
                dve.wait_ge(s["route"], g * ROUTE + 6)
                step(tt(t2[3][:, :, :], t2[1][:, :, :], t2[2][:, :, :], ALU.max))

            def route_group_score(g):
                hi, lo = t2[0], t2[3]
                dve.wait_ge(s["route"], g * ROUTE + 7)
                step(tt(t1[0][:, :, :], hi[:, :, 0:1], hi[:, :, 1:2], ALU.max))
                step(tt(t1[1][:, :, :], hi[:, :, 0:1], hi[:, :, 1:2], ALU.min))
                step(tt(t1[2][:, :, :], lo[:, :, 0:1], lo[:, :, 1:2], ALU.max))
                dve.wait_ge(s["route"], g * ROUTE + 10)
                step(tt(t1[3][:, :, :], t1[1][:, :, :], t1[2][:, :, :], ALU.max))
                dve.wait_ge(s["route"], g * ROUTE + 11)
                step(tt(gscore[:, :, :], t1[0][:, :, :], t1[3][:, :, :], ALU.add))

            def route_group_rank(g):
                v = gscore[:, :, :].rearrange("p (t a) o -> p t (a o)", t=TB)
                other = v.unsqueeze(2).broadcast_to([P, TB, G, G])
                own = v.unsqueeze(3).broadcast_to([P, TB, G, G])
                dve.wait_ge(s["route"], g * ROUTE + 12)
                step(tt(gcmp[0][:, :, :, :], other, own, ALU.is_gt))
                step(tt(gcmp[1][:, :, :, :], other, own, ALU.is_equal))
                dve.wait_ge(s["route"], g * ROUTE + 14)
                step(tt(gcmp[2][:, :, :, :], gcmp[1][:, :, :, :], tie, ALU.mult))
                dve.wait_ge(s["route"], g * ROUTE + 15)
                step(tt(gcmp[1][:, :, :, :], gcmp[0][:, :, :, :], gcmp[2][:, :, :, :], ALU.add))

            def route_mask(g):
                dve.wait_ge(s["route"], g * ROUTE + 16)
                step(nc.vector.tensor_reduce(grank[:, :, 0], gcmp[1][:, :, :, :]
                                             .rearrange("p t a b -> p (t a) b"), AX.X, ALU.add))
                dve.wait_ge(s["route"], g * ROUTE + 17)
                step(nc.vector.tensor_scalar(gpen[:, :, :], grank[:, :, :], 1.5, NEG,
                                             ALU.is_gt, ALU.mult))
                dve.wait_ge(s["route"], g * ROUTE + 18)
                step(tt(masked[:, :, :].rearrange("p t (a b) -> p (t a) b", a=G),
                        sc[:, :, :].rearrange("p t (a b) -> p (t a) b", a=G),
                        gpen[:, :, :].broadcast_to([P, TB * G, EG]), ALU.add))

            def route_topk(g):
                dve.wait_ge(s["route"], g * ROUTE + 19)
                nc.vector.tensor_copy(pace[:, :], ident[:, 0:1])
                for t in range(TB):
                    step(nc.vector.max(top[:, t, :], masked[:, t, :]))

            def route_places(g):
                dve.wait_ge(s["route"], g * ROUTE + 23)
                nc.vector.tensor_copy(pace[:, :], ident[:, 0:1])
                for t in range(TB):
                    step(nc.vector.max_index(topi[:, t, :], top[:, t, :], masked[:, t, :]))
                dve.wait_ge(s["route"], g * ROUTE + 27)
                step(nc.vector.tensor_copy(topf[:, :, :], topi[:, :, :]))

            def route_onehot(g):
                dve.wait_ge(s["route"], g * ROUTE + 28)
                step(tt(onehot[:, :, :, :], iota.unsqueeze(1).broadcast_to([P, TB, E, TOPK]),
                        topf[:, :, 0:TOPK].unsqueeze(2).broadcast_to([P, TB, E, TOPK]),
                        ALU.is_equal))

            def route_chosen(g):
                dve.wait_ge(s["route"], g * ROUTE + 29)
                step(nc.vector.tensor_reduce(chosen[:, :, :], onehot[:, :, :, :], AX.X, ALU.add))
                step(tt(anch[:, :, :], onehot[:, :, 0:E:2, 0], onehot[:, :, 1:E:2, 0], ALU.add))

            def route_weights(g):
                dve.wait_ge(s["route"], g * ROUTE + 31)
                step(tt(wts[:, :, :], chosen[:, :, :], score[:, :, :], ALU.mult))
                step(nc.vector.tensor_scalar(cw[:, :, E:E + L], anch[:, :, :], 0.05, None, ALU.mult))
                dve.wait_ge(s["route"], g * ROUTE + 33)
                step(nc.vector.tensor_reduce(wsum[:, :, 0], wts[:, :, :], AX.X, ALU.add))
                dve.wait_ge(s["route"], g * ROUTE + 34)
                step(nc.vector.tensor_scalar(wsum_e[:, :, :], wsum[:, :, :], 1e-20, None, ALU.add))

            def route_scale(g):
                dve.wait_ge(s["route"], g * ROUTE + 35)
                step(nc.vector.reciprocal(wrec[:, :, :], wsum_e[:, :, :]))
                dve.wait_ge(s["route"], g * ROUTE + 36)
                step(nc.vector.tensor_scalar(wfac[:, :, :], wrec[:, :, :], 0.1, None, ALU.mult))
                dve.wait_ge(s["route"], g * ROUTE + 37)
                step(tt(cw[:, :, 0:E], wts[:, :, :], wfac[:, :, :].broadcast_to([P, TB, E]), ALU.mult))

            def route_parts(g, first):
                dve.wait_ge(s["route"], g * ROUTE + 38)
                if not first:
                    dve.wait_ge(s["cwT_ps"], g)
                step(nc.vector.tensor_copy(cw2[:, :, 0:ROWS].bitcast(F32R), cw[:, :, :]))
                dve.wait_ge(s["route"], g * ROUTE + 39)
                step(tt(cw2[:, :, ROWS:], cw[:, :, :], cw2[:, :, 0:ROWS], ALU.subtract))

            ROUTING = {7: route_scores, 8: route_top2, 9: route_group_score, 10: route_group_rank,
                       11: route_mask, 12: route_topk, 13: route_places, 14: route_onehot,
                       15: route_chosen, 16: route_weights, 17: route_scale}

            def xT_low(g, first=False):
                if not first:
                    dve.wait_ge(s["gate_up_ps"], g * HT)
                dve.wait_ge(s["xT_hi"], g + 1)
                tt(xTp[1][:, :], xT[:, :], f32(xTp[0][:, :]), ALU.subtract).then_inc(s["xT_lo"], 1)

            def add_y(g, stats_before):
                c = g if stats_before is not None else g - NC
                xs = x[:, bass.ds(c * TB, TB), :]
                dve.wait_ge(s["yT_ps"], g + 1)
                tt(xs, xs, psM[:, :].rearrange("p (t d) -> p t d", t=TB), ALU.add) \
                    .then_inc(s["x_added"], 1)
                if stats_before is not None:
                    dve.wait_ge(s["x_added"], g + 1)
                    chunk_stats(c, c + stats_before)

            def ffn_chunk(g, g0, first, last, before):
                for j in range(HT):
                    if j == 0 and not last:
                        dve.wait_ge(s["xT_ps"], g + 1)
                        normalise(g + 1 - g0, "xn_ready")
                    dve.wait_ge(s["silu_done"], tiles(g, j))
                    if not (first and j < 3):
                        dve.wait_ge(s["z_lo"], tiles(g, j) - 3)
                    tt(z[j % 3], psU[j % 2][:, :], silu[j % 2], ALU.mult).then_inc(s["gated_done"], 1)
                    if j == 9 and not first:
                        add_y(g - 1, before)
                    if j in ROUTING and not last:
                        ROUTING[j](g + 1)
                    if j == 18 and not last:
                        route_parts(g + 1, False)
                    dve.wait_ge(s["gated_done"], tiles(g, j))
                    dve.wait_ge(s["spread_ps"], tiles(g, j))
                    tt(z[j % 3], z[j % 3], psW[j % 2][:, :], ALU.mult).then_inc(s["z_done"], 1)
                if not last:
                    xT_low(g + 1)

            def ffn(g0, before):
                normalise(0, "xn_ready")
                for k in ROUTING:
                    ROUTING[k](g0)
                route_parts(g0, g0 == 0)
                xT_low(g0, g0 == 0)
                ffn_chunk(g0, g0, True, False, before)
                with dve.Fori(g0 + 1, g0 + NC - 1) as g:
                    ffn_chunk(g, g0, False, False, before)
                ffn_chunk(g0 + NC - 1, g0, False, True, before)
                add_y(g0 + NC - 1, before)

            def a_rows(b, first):
                if not first:
                    dve.wait_ge(s["a_xT_ps"], b)
                    dve.wait_ge(s["a_xn_lo"], b)
                normalise(b, "a_xn")
                dve.wait_ge(s["a_xn"], b + 1)
                xs = x[:, bass.ds(b * TB, TB), :]
                tt(xs, xs, xn[:, :, :], ALU.add).then_inc(s["a_xres"], 1)

            def a_xT_low(b, first):
                if not first:
                    dve.wait_ge(s["yh_ps"], b * H)
                    dve.wait_ge(s["s_ps"], b * H * TB)
                dve.wait_ge(s["a_xT_hi"], b + 1)
                tt(xTp[1][:, :], xT[:, :], f32(xTp[0][:, :]), ALU.subtract) \
                    .then_inc(s["a_xT_lo"], 1)

            def a_row_parts(b, first):
                if not first:
                    dve.wait_ge(s["ctx_ps"], b * H)
                nc.vector.tensor_copy(xnp[0][:, :, :], xn[:, :, :]).then_inc(s["a_xn_hi"], 1)
                dve.wait_ge(s["a_xn_hi"], b + 1)
                tt(xnp[1][:, :, :], xn[:, :, :], f32(xnp[0][:, :, :]), ALU.subtract) \
                    .then_inc(s["a_xn_lo"], 1)

            def y_lo(b, h):
                n = b * H + h
                dve.wait_ge(s["yh_hi"], n + 1)
                tt(yh[1][:, h % 2, :], psYh[:, :], f32(yh[0][:, h % 2, :]), ALU.subtract) \
                    .then_inc(s["yh_lo"], 1)

            def row_max(b, h, qb):
                n = b * H + h
                dve.wait_ge(s["s_ps"], n * TB + TB - qb)
                nc.vector.tensor_reduce(nmax[:, h % 2, qb:qb + 1], psS[qb % 2][:, 0:(qb + 1) * P],
                                        AX.X, ALU.max, negate=True).then_inc(s["max_done"], 1)

            def pT_lo(b, h, part):
                n = b * H + h
                dve.wait_ge(s["pT_hi"], n * 3 + part + 1)
                o, w = ((0, 512), (640, 512), (1152, 256))[part]
                tt(pT[1][:, h % 2, o:o + w], psPT[part][:, 0:w], f32(pT[0][:, h % 2, o:o + w]),
                   ALU.subtract).then_inc(s["pT_lo"], 1)

            def norm(b, h):
                n = b * H + h
                dve.wait_ge(s["exp_done"], n * TB + TB)
                nc.vector.reciprocal(rrec[:, h % 2, :], rsum[:, h % 2, :]).then_inc(s["rec_done"], 1)
                dve.wait_ge(s["rec_done"], n + 1)
                for qb in (3, 2, 1, 0):
                    o = qb * (qb + 1) // 2 * P
                    p = prob[:, h % 2, o:o + (qb + 1) * P]
                    nc.vector.tensor_scalar(p, p, rrec[:, h % 2, qb:qb + 1], None, ALU.mult) \
                        .then_inc(s["norm_done"], 1)

            def add_out(b):
                dve.wait_ge(s["out_ps"], b * H + H)
                dve.wait_ge(s["a_xres"], b + 1)
                xs = x[:, bass.ds(b * TB, TB), :]
                tt(xs, xs, psO[:, :].rearrange("p (t d) -> p t d", t=TB), ALU.add) \
                    .then_inc(s["out_added"], 1)
                dve.wait_ge(s["out_added"], b + 1)
                chunk_stats(b, b + 2 * NC)

            def attn_slot(b, sl, first, last):
                nxt = lambda k: (b, sl + k) if sl + k < H else (b + 1, sl + k - H)
                have_y = not (last and sl + 2 >= H)
                have_s = not (last and sl + 1 >= H)
                if have_s:
                    row_max(*nxt(1), 3)
                if have_y and sl + 2 != H:
                    y_lo(*nxt(2))
                if sl == 2 and not first:
                    add_out(b - 1)
                if sl == 8 and not last:
                    a_rows(b + 1, False)
                pT_lo(b, sl, 0)
                if have_s:
                    row_max(*nxt(1), 2)
                pT_lo(b, sl, 1)
                if have_s:
                    row_max(*nxt(1), 1)
                    row_max(*nxt(1), 0)
                pT_lo(b, sl, 2)
                if have_y and sl + 2 == H:
                    a_xT_low(b + 1, False)
                if sl == 0 and not first:
                    a_row_parts(b, False)
                if have_s:
                    norm(*nxt(1))
                if have_y and sl + 2 == H:
                    y_lo(*nxt(2))

            def attention():
                for k in range(H // TB):
                    dve.wait_ge(s["mb_hi"], k + 1)
                    nc.vector.scalar_tensor_tensor(
                        out=head_columns(mh[1], k),
                        in0=psG[k % 2][:, :].rearrange("p (j d) -> p j d", d=P),
                        scalar=float(DK) ** -0.5, in1=f32(head_columns(mh[0], k)),
                        op0=ALU.mult, op1=ALU.subtract).then_inc(s["mb_lo"], 1)
                dve.wait_ge(s["down_ps"], NC * HT)
                for t in pT:
                    m = nc.vector.memset(t[:, :, 512:640].bitcast(F32), 0.0)
                m.then_inc(s["zeroed"], 1)
                finish_std(2)
                a_rows(0, True)
                a_xT_low(0, True)
                a_row_parts(0, True)
                y_lo(0, 0)
                for qb in (3, 2, 1, 0):
                    row_max(0, 0, qb)
                norm(0, 0)
                y_lo(0, 1)
                for sl in range(H):
                    attn_slot(0, sl, True, False)
                with dve.Fori(1, NC - 1) as b:
                    for sl in range(H):
                        attn_slot(b, sl, False, False)
                for sl in range(H):
                    attn_slot(NC - 1, sl, False, True)
                add_out(NC - 1)

            dve.wait_ge(s["consts_loaded"], 48)
            for c in range(NC):
                dve.wait_ge(x_loads[c], 16)
                chunk_stats(c, c)
            nc.vector.tensor_copy(half[:, :], small[:, 0:2 * P])
            nc.vector.memset(cw[:, :, E + L + 1:], 0.0)
            nc.vector.memset(cw[:, :, E + L:E + L + 1], 0.5).then_inc(s["cw_const"], 1)
            dve.wait_ge(s["cw_const"], 1)
            finish_std(1)
            for k in range(CONV_GROUPS):
                split_group_lo(k)
            ffn(0, NC)
            attention()
            finish_std(3)
            ffn(NC, None)

        @block.gpsimd
        def _(pool):
            pool.dma_start(sel[:, :], sel_in).then_inc(s["sel_loaded"], 16)

            def z_low(g, j):
                pool.wait_ge(s["z_hi"], tiles(g, j))
                nc.gpsimd.tensor_tensor(zp[1][part_slot(j)], z[j % 3], f32(zp[0][part_slot(j)]),
                                        ALU.subtract).then_inc(s["z_lo"], 1)

            for g0 in (0, NC):
                with pool.Fori(g0, g0 + NC) as g:
                    for j in range(HT):
                        z_low(g, j)


def kernel(L0_attn_x, L0_attn_Wq, L0_attn_Wk, L0_attn_Wv, L0_attn_Wo, L0_ffn_gate_weight,
           L0_ffn_gate_bias, L0_ffn_w_gate, L0_ffn_w_up, L0_ffn_w_down, L0_ffn_shared_w_gate,
           L0_ffn_shared_w_up, L0_ffn_shared_w_down, L0_ffn_anchor_w_gate, L0_ffn_anchor_w_up,
           L0_ffn_anchor_w_down):
    import concourse.bacc as bacc
    from concourse.bass_utils import run_bass_kernel_spmd

    x = np.asarray(L0_attn_x)
    B, S, D = x.shape

    def hidden_columns(experts, anchors, shared):
        parts = [np.asarray(w).transpose(1, 0, 2).reshape(D, -1) for w in (experts, anchors)]
        parts.append(np.asarray(shared))
        w = np.zeros((D, HT * P), np.float32)
        w[:, :sum(p.shape[1] for p in parts)] = np.concatenate(parts, 1)
        return w

    down = np.zeros((HT * P, D), np.float32)
    rows = np.concatenate([np.asarray(L0_ffn_w_down).reshape(-1, D),
                           np.asarray(L0_ffn_anchor_w_down).reshape(-1, D),
                           np.asarray(L0_ffn_shared_w_down)], 0)
    down[:rows.shape[0]] = rows
    small, sel = constants()
    arrays = {
        "x": x.reshape(B * S, D),
        "w_gate": hidden_columns(L0_ffn_w_gate, L0_ffn_anchor_w_gate, L0_ffn_shared_w_gate),
        "w_up": hidden_columns(L0_ffn_w_up, L0_ffn_anchor_w_up, L0_ffn_shared_w_up),
        "w_down": down.reshape(HT, P, D).transpose(1, 0, 2).reshape(P, HT * D),
        "gate_weight": np.asarray(L0_ffn_gate_weight).T,
        "gate_bias": np.asarray(L0_ffn_gate_bias),
        "wqT": np.asarray(L0_attn_Wq).T,
        "wkT": np.asarray(L0_attn_Wk).T,
        "wvT": np.asarray(L0_attn_Wv).T,
        "wo": np.asarray(L0_attn_Wo),
        "small": small, "sel": sel,
    }
    arrays = {n: np.ascontiguousarray(a) for n, a in arrays.items()}
    nc = bacc.Bacc("TRN2", target_bir_lowering=False, num_devices=1)
    args = [nc.dram_tensor("in_" + n, a.shape, mybir.dt.from_np(a.dtype), kind="ExternalInput").ap()
            for n, a in arrays.items()]
    out = nc.dram_tensor("out_rows", (B * S, D), F32, kind="ExternalOutput").ap()
    build(nc, *args, out)
    r = run_bass_kernel_spmd(nc, [{"in_" + n: a for n, a in arrays.items()}], core_ids=[0])
    return r.results[0]["out_rows"].reshape(B, S, D)
```

```python
from contextlib import ExitStack

import numpy as np

import concourse.bass as bass
from concourse import mybir

ALU = mybir.AluOpType
ACT = mybir.ActivationFunctionType
AX = mybir.AxisListType
F32 = mybir.dt.float32
F32R = mybir.dt.float32r
BF16 = mybir.dt.bfloat16
U32 = mybir.dt.uint32

P = 128
TB = 4
CH = TB * P
E, G, TOPK, MI = 32, 4, 6, 64
EG = E // G
L, AI = 16, 32
ROWS = 64
HT = (E * MI + L * AI + MI + P - 1) // P
H, DK = 16, 64
LAG = 3
NEG = -1.0e30
EPS = 1e-5
KB_OFF = [0, 640 + 128, 1152, 640]
PT_W = 1408
PW = TB * (TB + 1) // 2 * P
CONV_GROUPS = 3
GT = HT // CONV_GROUPS


def constants():
    ident = np.eye(P, dtype=np.float32)
    sel = np.zeros((P, HT, P), np.float32)
    for row in range(HT * P):
        if row < E * MI:
            src = row // MI
        elif row < E * MI + L * AI:
            src = E + (row - E * MI) // AI
        else:
            src = E + L
        sel[src, row // P, row % P] = 1.0
        sel[ROWS + src, row // P, row % P] = 1.0
    mask = np.where(np.arange(P)[None, :] > np.arange(P)[:, None], NEG, 0.0)
    iota = np.broadcast_to(np.arange(E, dtype=np.float32)[None, :, None], (P, E, TOPK))
    tie = np.broadcast_to((np.arange(G)[None, :] < np.arange(G)[:, None]), (P, TB, G, G))
    small = np.concatenate([ident, mask, iota.reshape(P, -1), tie.reshape(P, -1)], 1)
    return small.astype(np.float32), sel.reshape(P, -1)


def build(nc, x_in, wg_in, wu_in, wd_in, gate_in, bias_in, wqT_in, wkT_in, wvT_in, wo_in,
          small_in, sel_in, out):
    T = x_in.shape[0]
    NT = T // P
    NC = T // CH
    HC = HT * P
    ctx = ExitStack()
    with ctx:
        def sb(name, shape, dt=F32):
            return ctx.enter_context(nc.sbuf_tensor(name, shape, dt))

        def sem(name):
            return ctx.enter_context(nc.semaphore(name))

        small = sb("small", [P, 2 * P + E * TOPK + TB * G * G])
        ident = small[:, 0:P]
        iota = small[:, 2 * P:2 * P + E * TOPK].rearrange("p (e k) -> p e k", e=E)
        tie = small[:, 2 * P + E * TOPK:].rearrange("p (t a b) -> p t a b", t=TB, a=G)
        half = sb("half", [P, 2 * P], BF16)
        ident_bf, mask_bf = half[:, 0:P], half[:, P:2 * P]
        sel = sb("sel", [P, HC], F32R)
        gate_w = sb("gate_w", [P, E])
        bias = sb("bias", [P, E])
        wg = [sb(f"wg_{n}", [P, HC], F32R) for n in ("hi", "lo")]
        wu = [sb(f"wu_{n}", [P, HC], F32R) for n in ("hi", "lo")]
        wd = [sb(f"wd_{n}", [P, HC], F32R) for n in ("hi", "lo")]
        stage = sb("stage", [P, 2, 3, GT * P])
        attn_w = stage[:, :, :, :].rearrange("p a b c -> p (a b c)")[:, 0:4 * H * DK] \
            .rearrange("p (w j d) -> p w j d", w=4, j=H // 2)
        mh = [sb(f"m_{n}", [P, H * P], F32R) for n in ("hi", "lo")]
        bh = sb("b_h", [P, H * P])
        x = sb("x", [P, NT, P])
        bn = sb("bn", [P, TB, 6])
        mean_var = sb("mean_var", [P, TB, 2])
        mean = sb("mean", [P, NT])
        var_eps = sb("var_eps", [P, NT])
        std = sb("std", [P, NT])
        rstd0 = sb("rstd0", [P, NT])
        newton = sb("newton", [P, NT])
        pool_pace = sb("pool_pace", [P, 2 * TB])
        pace = sb("pace", [P, 1])
        rstd = sb("rstd", [P, NT])
        xn = sb("xn", [P, TB, P])
        xT_parts = [sb(f"xT_{n}", [P, 2 * CH], F32R) for n in ("hi", "lo")]
        score = sb("score", [P, TB, E])
        sc = sb("sc", [P, TB, E])
        t4 = [sb(f"t4_{i}", [P, TB * G, 4]) for i in range(2)]
        t2 = [sb(f"t2_{i}", [P, TB * G, 2]) for i in range(4)]
        t1 = [sb(f"t1_{i}", [P, TB * G, 1]) for i in range(4)]
        gscore = sb("gscore", [P, TB * G, 1])
        gcmp = [sb(f"gcmp_{i}", [P, TB, G, G]) for i in range(3)]
        grank = sb("grank", [P, TB * G, 1])
        gpen = sb("gpen", [P, TB * G, 1])
        masked = sb("masked", [P, TB, E])
        top = sb("top", [P, TB, 8])
        topi = sb("topi", [P, TB, 8], U32)
        topf = sb("topf", [P, TB, 8])
        onehot = sb("onehot", [P, TB, E, TOPK])
        chosen = sb("chosen", [P, TB, E])
        wts = sb("wts", [P, TB, E])
        wsum = sb("wsum", [P, TB, 1])
        wsum_e = sb("wsum_e", [P, TB, 1])
        wrec = sb("wrec", [P, TB, 1])
        wfac = sb("wfac", [P, TB, 1])
        anch = sb("anch", [P, TB, L])
        cw = sb("cw", [P, TB, ROWS])
        cw2 = sb("cw2", [P, TB, 2 * ROWS])
        prob = sb("prob", [P, 2, PW])
        pT = [sb(f"pT_{n}", [P, 2, PT_W], F32R) for n in ("hi", "lo")]
        yh = [sb(f"y_{n}", [P, 2, CH], F32R) for n in ("hi", "lo")]
        row_parts = sb("row_parts", [P, 2, TB, P], F32R)
        xnp = [row_parts[:, i, :, :] for i in (0, 1)]
        ctxT = sb("ctxT", [P, 2, CH])
        yT, xT = ctxT[:, 0, :], ctxT[:, 1, :]
        cwT_ring = row_parts[:, :, :, :].rearrange("p a b c -> p (a b c)")
        nmax = sb("nmax", [P, 2, TB])
        rsum = sb("rsum", [P, 2, TB])
        rrec = sb("rrec", [P, 2, TB])
        ffn_f = prob[:, :, :].rearrange("p a b -> p (a b)")
        silu = [ffn_f[:, i * CH:(i + 1) * CH] for i in (0, 1)]
        z = [ffn_f[:, i * CH:(i + 1) * CH] for i in (2, 3, 4)]
        NZ = 5
        pT_flat = [t[:, :, :].rearrange("p a b -> p (a b)") for t in pT]
        zp = [[t[:, i * CH:(i + 1) * CH] for i in range(NZ)] for t in pT_flat]

        bank = [ctx.enter_context(nc.psum_tensor(f"bank{i}", [P, 512], F32)) for i in range(8)]
        psG, psU, psW, psY, psM = bank[0:2], bank[2:4], bank[4:6], bank[6], bank[7]
        psS, psPT, psYh, psC, psO = bank[0:3], [bank[3], bank[4], bank[3]], bank[5], bank[6], bank[7]

        names = """consts_loaded sel_loaded attn_w_loaded
            wsplit_hi wsplit_lo stat_dve stat_act stat_rows stat_bn cw_const
            xn_ready xT_ps xT_sb logits_ps sigmoid_done route cwT_ps cwT_sb xT_hi xT_lo
            gate_up_ps spread_ps silu_done gated_done z_done z_hi z_lo down_ps
            y_evac yT_ps x_added
            mb_ps mb_hi mb_lo zeroed
            a_xn a_xT_ps a_xT_sb a_xT_hi a_xT_lo a_xres a_xn_hi a_xn_lo
            yh_ps yh_hi yh_lo s_ps max_done exp_done rec_done norm_done
            pT_ps pT_hi pT_lo ctx_ps ctx_sb out_ps out_added stored""".split()
        s = {n: sem("s_" + n) for n in names}
        x_loads = [sem(f"s_x_load{c}") for c in range(NC)]
        w_loads = [sem(f"s_w_load{k}") for k in range(CONV_GROUPS)]

        block = ctx.enter_context(nc.Block())

        def f32(ap):
            return ap.bitcast(F32)

        def mm3(pe, o, w, m, start, stop):
            pe.matmul(o, w[0], m[0], start=start, stop=False, skip_group_check=True)
            pe.matmul(o, w[0], m[1], start=False, stop=False, skip_group_check=True)
            return pe.matmul(o, w[1], m[0], start=False, stop=stop, skip_group_check=True)

        def of_chunk(ring, c, o=0, w=CH):
            if isinstance(c, int):
                return ring[:, (c % 2) * CH + o:(c % 2) * CH + o + w]
            return ring[:, bass.ds((c % 2) * CH + o, w)]

        def tiles(g, j):
            return g * HT + j + 1

        def two_ago(g, j):
            return g * HT + (j - 1 if j > 1 else -j)

        def part_slot(j):
            return j % 4 if j < HT - 1 else 4

        def part_slot_free(g, j):
            return tiles(g, j) - (HT if j == HT - 1 else 4 if j > 3 else 5)

        ROUTE = 40

        def weight_heads(k):
            k %= H // TB
            return [(k // 2) * 2 * TB + 2 * i + k % 2 for i in range(TB)]

        def head_columns(t, k):
            h = weight_heads(k)[0]
            return t[:, :].rearrange("p (j two d) -> p j two d", two=2, d=P)[:, h // 2:h // 2 + TB, h % 2, :]

        def scores_of(qb):
            o = 2 * P if qb == 0 else 0
            return psS[(2, 2, 1, 0)[qb]][:, o:o + (qb + 1) * P]

        @block.sync
        def _(sp):
            def load_group(sp, k):
                cols = slice(k * GT * P, (k + 1) * GT * P)
                for w, src in enumerate((wg_in, wu_in, wd_in)):
                    sp.dma_start(stage[:, k % 2, w, :], src[:, cols]).then_inc(w_loads[k], 16)

            sp.dma_start(small[:, :], small_in).then_inc(s["consts_loaded"], 16)
            sp.dma_start(gate_w[:, :], gate_in).then_inc(s["consts_loaded"], 16)
            sp.dma_start(bias[:, :], bias_in.partition_broadcast(P)).then_inc(s["consts_loaded"], 16)
            for c in range(NC):
                sp.dma_start(x[:, c * TB:(c + 1) * TB, :],
                             x_in[c * CH:(c + 1) * CH, :].rearrange("(t p) d -> p t d", p=P)) \
                    .then_inc(x_loads[c], 16)
                if c < 2:
                    load_group(sp, c)
            for k in range(2, CONV_GROUPS):
                sp.wait_ge(s["wsplit_lo"], 3 * (k - 1))
                load_group(sp, k)
            sp.wait_ge(s["wsplit_lo"], 3 * CONV_GROUPS)
            for w, src in enumerate((wqT_in, wkT_in, wvT_in, wo_in)):
                sp.dma_start(attn_w[:, w, :, :], src.rearrange("(j p) d -> p j d", p=P)) \
                    .then_inc(s["attn_w_loaded"], 16)
            with sp.Fori(0, NC) as c:
                sp.wait_ge(s["x_added"], (c + NC) + 1)
                sp.dma_start(out[bass.ds(c * CH, CH), :].rearrange("(t p) d -> p t d", p=P),
                             x[:, bass.ds(c * TB, TB), :]).then_inc(s["stored"], 16)
            sp.wait_ge(s["stored"], 16 * NC)

        @block.tensor
        def _(pe):
            def to_columns(dst, src, n=TB):
                for t in range(n):
                    m = pe.transpose(dst[:, t * P:(t + 1) * P], src[:, t, :], ident)
                return m

            def prep_xT(g):
                pe.wait_ge(s["xn_ready"], g + 1)
                to_columns(psM, xn).then_inc(s["xT_ps"], 1)

            def prep_logits(g):
                pe.wait_ge(s["xT_hi"], g + 1)
                for t in range(TB):
                    m = pe.matmul(psM[:, t * E:(t + 1) * E], xT[:, t * P:(t + 1) * P], gate_w[:, :],
                                  start=True, stop=True, skip_group_check=True)
                m.then_inc(s["logits_ps"], 1)

            def prep_cwT(g):
                pe.wait_ge(s["route"], (g + 1) * ROUTE)
                to_columns(psM, cw2).then_inc(s["cwT_ps"], 1)

            def gate_up(g, j, first):
                if j == 0:
                    pe.wait_ge(s["xT_lo"], g + 1)
                if not (first and j < 2):
                    pe.wait_ge(s["gated_done"], two_ago(g, j))
                c = slice(j * P, (j + 1) * P)
                xp = [of_chunk(t, g) for t in xT_parts]
                mm3(pe, psG[j % 2][:, :], [w[:, c] for w in wg], xp, True, True)
                mm3(pe, psU[j % 2][:, :], [w[:, c] for w in wu], xp, True, True) \
                    .then_inc(s["gate_up_ps"], 1)

            def spread(g, j, first):
                if j == 0:
                    pe.wait_ge(s["cwT_sb"], g + 1)
                if not (first and j < 2):
                    pe.wait_ge(s["z_done"], two_ago(g, j))
                pe.matmul(psW[j % 2][:, :], sel[:, j * P:(j + 1) * P], of_chunk(cwT_ring, g),
                          start=True, stop=True).then_inc(s["spread_ps"], 1)

            def down(g, j, first):
                pe.wait_ge(s["z_lo"], tiles(g, j))
                if j == 0 and not first:
                    pe.wait_ge(s["y_evac"], g)
                c = slice(j * P, (j + 1) * P)
                mm3(pe, psY[:, :], [w[:, c] for w in wd], [zp[0][part_slot(j)], zp[1][part_slot(j)]],
                    j == 0, j == HT - 1).then_inc(s["down_ps"], 1)

            def post_yT(g):
                pe.wait_ge(s["y_evac"], g + 1)
                to_columns(psM, yT.rearrange("p (t d) -> p t d", t=TB)).then_inc(s["yT_ps"], 1)

            def ffn_chunk(g, first, last, setup=False):
                for j in range(HT):
                    if setup and j % GT == 0:
                        pe.wait_ge(s["wsplit_lo"], 3 * (j // GT + 1))
                        pe.wait_ge(s["wsplit_hi"], 3 * (j // GT + 1))
                    if j == 2 and not last:
                        prep_xT(g + 1)
                    if j == 4 and not last:
                        prep_logits(g + 1)
                    if j == 7 and not first:
                        if not last:
                            pe.wait_ge(s["sigmoid_done"], g + 2)
                        post_yT(g - 1)
                    if j == HT - 1 and not last:
                        if not first:
                            pe.wait_ge(s["x_added"], g)
                        else:
                            pe.wait_ge(s["sigmoid_done"], g + 2)
                        prep_cwT(g + 1)
                    gate_up(g, j, first)
                    spread(g, j, first)
                    if j >= LAG:
                        down(g, j - LAG, first)
                    elif not first:
                        down(g - 1, HT - LAG + j, False)

            def ffn(g0):
                prep_xT(g0)
                prep_logits(g0)
                pe.wait_ge(s["sigmoid_done"], g0 + 1)
                prep_cwT(g0)
                if g0 == 0:
                    pe.wait_ge(s["sel_loaded"], 16)
                ffn_chunk(g0, True, False, setup=g0 == 0)
                with pe.Fori(g0 + 1, g0 + NC - 1) as g:
                    ffn_chunk(g, False, False)
                ffn_chunk(g0 + NC - 1, False, True)
                for j in range(HT - LAG, HT):
                    down(g0 + NC - 1, j, False)
                pe.wait_ge(s["x_added"], g0 + NC - 1)
                post_yT(g0 + NC - 1)

            def a_prep(b):
                pe.wait_ge(s["a_xn"], b + 1)
                to_columns(psYh, xn).then_inc(s["a_xT_ps"], 1)

            def head_y(b, h):
                n = b * H + h
                if h == 0:
                    pe.wait_ge(s["a_xT_lo"], b + 1)
                if not (isinstance(b, int) and n == 0):
                    pe.wait_ge(s["yh_lo"], n)
                c = slice(h * P, (h + 1) * P)
                mm3(pe, psYh[:, :], [w[:, c] for w in mh], [of_chunk(t, b) for t in xT_parts],
                    True, True).then_inc(s["yh_ps"], 1)

            def head_scores(b, h, u, first):
                n = b * H + h
                if u == 0:
                    pe.wait_ge(s["yh_lo"], n + 1)
                if not (first and h == 0):
                    pe.wait_ge(s["exp_done"], (n - 1) * TB + (1, 2, 4)[u])
                for qb in ((3,), (2,), (1, 0))[u]:
                    w = max(2, qb + 1) * P
                    o = 2 * P if qb == 0 else 0
                    q = slice(qb * P, (qb + 1) * P)
                    mm3(pe, psS[u][:, o:o + w], [t[:, h % 2, q] for t in yh],
                        [of_chunk(t, b, 0, w) for t in xT_parts], True, False)
                    m = pe.matmul(psS[u][:, o + qb * P:o + (qb + 1) * P], ident_bf, mask_bf,
                                  start=False, stop=True, skip_group_check=True)
                m.then_inc(s["s_ps"], 1)

            def head_probT(b, h, part, first):
                n = b * H + h
                if part == 0:
                    pe.wait_ge(s["norm_done"], n * TB + TB)
                if part == 2:
                    pe.wait_ge(s["pT_lo"], n * 3 + 1)
                elif not (first and h == 0):
                    pe.wait_ge(s["pT_lo"], (n - 1) * 3 + (3 if part == 0 else 2))
                blocks = [[(0, q) for q in range(TB)],
                          [(3, 3)] + [(1, q) for q in range(1, TB)],
                          [(2, q) for q in range(2, TB)]][part]
                for i, (kb, q) in enumerate(blocks):
                    o = q * (q + 1) // 2 * P + kb * P
                    m = pe.transpose(psPT[part][:, i * P:(i + 1) * P], prob[:, h % 2, o:o + P], ident)
                m.then_inc(s["pT_ps"], 1)

            def head_pv(b, h, kb, first):
                n = b * H + h
                if kb == 0:
                    pe.wait_ge(s["pT_lo"], n * 3 + 3)
                    if h == 0:
                        pe.wait_ge(s["a_xn_lo"], b + 1)
                    if not (first and h == 0):
                        pe.wait_ge(s["ctx_sb"], n)
                q0 = min(kb, TB - 2) * P
                o = KB_OFF[kb] - (P if kb == 3 else 0)
                w = CH - q0
                m = mm3(pe, psC[:, q0:CH], [t[:, kb, :] for t in xnp],
                        [t[:, h % 2, o:o + w] for t in pT], kb == 0, kb == 3)
                if kb == 3:
                    m.then_inc(s["ctx_ps"], 1)

            def head_out(b, h, first):
                n = b * H + h
                pe.wait_ge(s["ctx_sb"], n + 1)
                if h == 0 and not first:
                    pe.wait_ge(s["out_added"], b)
                for t in range(TB):
                    m = pe.matmul(psO[:, t * P:(t + 1) * P], ctxT[:, h % 2, t * P:(t + 1) * P],
                                  bh[:, h * P:(h + 1) * P], start=(h == 0 and t == 0),
                                  stop=(h == H - 1 and t == TB - 1), skip_group_check=True)
                m.then_inc(s["out_ps"], 1)

            def attn_slot(b, sl, first, last):
                nxt = lambda k: (b, sl + k) if sl + k < H else (b + 1, sl + k - H)
                prv = lambda k: (b, sl - k) if sl >= k else (b - 1, sl - k + H)
                have_y = not (last and sl + 2 >= H)
                have_s = not (last and sl + 1 >= H)
                have_v = not (first and sl < 1)
                have_o = not (first and sl < 2)
                if have_s:
                    for u in range(3):
                        head_scores(*nxt(1), u, False)
                if sl == 9 and not last:
                    pe.wait_ge(s["a_xT_lo"], b + 2)
                if have_y:
                    head_y(*nxt(2))
                if have_v:
                    for kb in range(TB):
                        head_pv(*prv(1), kb, first and sl < 2)
                head_probT(b, sl, 0, first)
                head_probT(b, sl, 1, first)
                if sl == 8 and not last:
                    pe.wait_ge(s["yh_lo"], b * H + 11)
                    a_prep(b + 1)
                if have_o:
                    head_out(*prv(2), first and sl - 2 < H)
                head_probT(b, sl, 2, first)

            def attention():
                pe.wait_ge(s["attn_w_loaded"], 64)
                for k in range(2 * H // TB):
                    if k == 0:
                        pe.wait_ge(s["gated_done"], NC * HT)
                    if k > 1:
                        pe.wait_ge(s["mb_hi"], k - 1)
                        pe.wait_ge(s["mb_lo"], min(k - 1, H // TB))
                    for i in range(TB):
                        h = weight_heads(k)[i]
                        r = slice((h % 2) * DK, (h % 2) * DK + DK)
                        a, c = (0, 1) if k < H // TB else (2, 3)
                        m = pe.matmul(psG[k % 2][:, i * P:(i + 1) * P], attn_w[r, a, h // 2, :],
                                      attn_w[r, c, h // 2, :], start=True, stop=True,
                                      skip_group_check=True)
                    m.then_inc(s["mb_ps"], 1)
                pe.wait_ge(s["x_added"], NC)
                a_prep(0)
                pe.wait_ge(s["zeroed"], 1)
                pe.wait_ge(s["cw_const"], 1)
                pe.wait_ge(s["mb_hi"], 2 * H // TB)
                pe.wait_ge(s["mb_lo"], H // TB)
                head_y(0, 0)
                for u in range(3):
                    head_scores(0, 0, u, True)
                head_y(0, 1)
                for sl in range(H):
                    attn_slot(0, sl, True, False)
                with pe.Fori(1, NC - 1) as b:
                    for sl in range(H):
                        attn_slot(b, sl, False, False)
                for sl in range(H):
                    attn_slot(NC - 1, sl, False, True)
                for kb in range(TB):
                    head_pv(NC - 1, H - 1, kb, False)
                head_out(NC - 1, H - 2, False)
                head_out(NC - 1, H - 1, False)
                pe.wait_ge(s["out_added"], NC)

            ffn(0)
            attention()
            ffn(NC)

        @block.scalar
        def _(act):
            def row_std(n):
                act.wait_ge(s["stat_bn"], n * NC)
                nc.scalar.activation(std[:, :], var_eps[:, :], ACT.Sqrt).then_inc(s["stat_act"], 1)

            def prep_copy(g):
                act.wait_ge(s["xT_ps"], g + 1)
                nc.scalar.activation(xT, psM[:, :], ACT.Copy).then_inc(s["xT_sb"], 1)
                nc.scalar.activation(of_chunk(xT_parts[0], g), psM[:, :], ACT.Copy) \
                    .then_inc(s["xT_hi"], 1)

            def prep_sigmoid(g, first=False):
                act.wait_ge(s["logits_ps"], g + 1)
                if not first:
                    act.wait_ge(s["route"], g * ROUTE)
                nc.scalar.activation(score[:, :, :].rearrange("p t e -> p (t e)"), psM[:, 0:TB * E],
                                     ACT.Sigmoid).then_inc(s["sigmoid_done"], 1)

            def prep_cwT(g):
                act.wait_ge(s["cwT_ps"], g + 1)
                nc.scalar.activation(of_chunk(cwT_ring, g), psM[:, :], ACT.Copy) \
                    .then_inc(s["cwT_sb"], 1)

            def z_hi(g, j, early):
                act.wait_ge(s["z_done"], tiles(g, j))
                if not early:
                    act.wait_ge(s["down_ps"], part_slot_free(g, j))
                nc.scalar.activation(zp[0][part_slot(j)], z[j % 3], ACT.Copy).then_inc(s["z_hi"], 1)

            def y_copy(g):
                act.wait_ge(s["down_ps"], tiles(g, HT - 1))
                nc.scalar.activation(yT, psY[:, :], ACT.Copy).then_inc(s["y_evac"], 1)

            def split_group_hi(k):
                act.wait_ge(w_loads[k], 48)
                c = slice(k * GT * P, (k + 1) * GT * P)
                for w, dst in enumerate((wg, wu, wd)):
                    nc.scalar.activation(dst[0][:, c], stage[:, k % 2, w, :], ACT.Copy) \
                        .then_inc(s["wsplit_hi"], 1)

            def ffn_chunk(g, first, last, setup=False):
                for j in range(HT):
                    if j == 3 and not last:
                        prep_copy(g + 1)
                    if j == 3 and not first:
                        y_copy(g - 1)
                    if j == 5 and not last:
                        prep_sigmoid(g + 1)
                    act.wait_ge(s["gate_up_ps"], tiles(g, j))
                    if not (first and j < 2):
                        act.wait_ge(s["gated_done"], two_ago(g, j))
                    nc.scalar.activation(silu[j % 2], psG[j % 2][:, :], ACT.Silu) \
                        .then_inc(s["silu_done"], 1)
                    if j > 0:
                        z_hi(g, j - 1, first and (j - 1 < 4 or j == HT))
                    elif not first:
                        z_hi(g - 1, HT - 1, False)
                if not last:
                    prep_cwT(g + 1)

            def ffn(g0):
                prep_copy(g0)
                prep_sigmoid(g0, g0 == 0)
                prep_cwT(g0)
                ffn_chunk(g0, True, False)
                with act.Fori(g0 + 1, g0 + NC - 1) as g:
                    ffn_chunk(g, False, False)
                ffn_chunk(g0 + NC - 1, False, True)
                z_hi(g0 + NC - 1, HT - 1, False)
                y_copy(g0 + NC - 1)

            def a_xT_high(b):
                act.wait_ge(s["a_xT_ps"], b + 1)
                nc.scalar.activation(of_chunk(xT_parts[0], b), psYh[:, :], ACT.Copy) \
                    .then_inc(s["a_xT_hi"], 1)

            def y_hi(b, h, early):
                n = b * H + h
                act.wait_ge(s["yh_ps"], n + 1)
                if not early:
                    act.wait_ge(s["s_ps"], (n - 1) * 3)
                nc.scalar.activation(yh[0][:, h % 2, :], psYh[:, :], ACT.Copy).then_inc(s["yh_hi"], 1)

            def exp(b, h, qb, early):
                n = b * H + h
                act.wait_ge(s["max_done"], n * TB + (4, 4, 2, 1)[qb])
                if not early:
                    act.wait_ge(s["pT_ps"], (n - 1) * 3)
                o = qb * (qb + 1) // 2 * P
                w = (qb + 1) * P
                nc.scalar.activation(prob[:, h % 2, o:o + w], scores_of(qb), ACT.Exp,
                                     bias=nmax[:, h % 2, qb:qb + 1],
                                     accum_out=rsum[:, h % 2, qb:qb + 1]).then_inc(s["exp_done"], 1)

            def pT_hi(b, h, part, early):
                n = b * H + h
                act.wait_ge(s["pT_ps"], n * 3 + part + 1)
                if not early:
                    act.wait_ge(s["ctx_ps"], n - 1)
                o, w = ((0, 512), (640, 512), (1152, 256))[part]
                nc.scalar.activation(pT[0][:, h % 2, o:o + w], psPT[part][:, 0:w], ACT.Copy) \
                    .then_inc(s["pT_hi"], 1)

            def ctx_copy(b, h, early):
                n = b * H + h
                act.wait_ge(s["ctx_ps"], n + 1)
                if not early:
                    act.wait_ge(s["out_ps"], n - 1)
                nc.scalar.activation(ctxT[:, h % 2, :], psC[:, :], ACT.Copy).then_inc(s["ctx_sb"], 1)

            def attn_slot(b, sl, first, last):
                nxt = lambda k: (b, sl + k) if sl + k < H else (b + 1, sl + k - H)
                prv = lambda k: (b, sl - k) if sl >= k else (b - 1, sl - k + H)
                have_y = not (last and sl + 2 >= H)
                have_s = not (last and sl + 1 >= H)
                early = first and sl < 1
                if have_s:
                    for qb in (3, 2, 1, 0):
                        exp(*nxt(1), qb, early)
                if have_y:
                    y_hi(*nxt(2), False)
                if not (first and sl < 1):
                    ctx_copy(*prv(1), first and sl < 3)
                pT_hi(b, sl, 0, first and sl < 2)
                pT_hi(b, sl, 1, first and sl < 2)
                if sl == 8 and not last:
                    a_xT_high(b + 1)
                pT_hi(b, sl, 2, first and sl < 2)

            def attention():
                for k in range(2 * H // TB):
                    act.wait_ge(s["mb_ps"], k + 1)
                    src = psG[k % 2][:, :].rearrange("p (j d) -> p j d", d=P)
                    if k < H // TB:
                        nc.scalar.activation(head_columns(mh[0], k), src, ACT.Copy,
                                             scale=float(DK) ** -0.5).then_inc(s["mb_hi"], 1)
                    else:
                        nc.scalar.activation(head_columns(bh, k), src, ACT.Copy) \
                            .then_inc(s["mb_hi"], 1)
                row_std(2)
                a_xT_high(0)
                y_hi(0, 0, True)
                for qb in (3, 2, 1, 0):
                    exp(0, 0, qb, True)
                y_hi(0, 1, True)
                for sl in range(H):
                    attn_slot(0, sl, True, False)
                with act.Fori(1, NC - 1) as b:
                    for sl in range(H):
                        attn_slot(b, sl, False, False)
                for sl in range(H):
                    attn_slot(NC - 1, sl, False, True)
                ctx_copy(NC - 1, H - 1, False)

            row_std(1)
            split_group_hi(0)
            for k in range(1, CONV_GROUPS):
                split_group_hi(k)
            ffn(0)
            attention()
            row_std(3)
            ffn(NC)

        @block.vector
        def _(dve):
            def finish_std(n):
                k = (n - 1) * 5
                dve.wait_ge(s["stat_act"], n)
                nc.vector.reciprocal(rstd0[:, :], std[:, :]).then_inc(s["stat_dve"], 1)
                dve.wait_ge(s["stat_dve"], k + 1)
                nc.vector.tensor_tensor(newton[:, :], rstd0[:, :], rstd0[:, :], ALU.mult) \
                    .then_inc(s["stat_dve"], 1)
                dve.wait_ge(s["stat_dve"], k + 2)
                nc.vector.tensor_tensor(newton[:, :], newton[:, :], var_eps[:, :], ALU.mult) \
                    .then_inc(s["stat_dve"], 1)
                dve.wait_ge(s["stat_dve"], k + 3)
                nc.vector.tensor_scalar(newton[:, :], newton[:, :], -0.5, 1.5, ALU.mult, ALU.add) \
                    .then_inc(s["stat_dve"], 1)
                dve.wait_ge(s["stat_dve"], k + 4)
                nc.vector.tensor_tensor(rstd[:, :], rstd0[:, :], newton[:, :], ALU.mult) \
                    .then_inc(s["stat_dve"], 1)
                dve.wait_ge(s["stat_dve"], k + 5)

            def chunk_stats(c, k):
                nc.vector.tensor_copy(pace[:, :], ident[:, 0:1])
                for t in range(TB):
                    m = nc.vector.bn_stats(bn[:, t, :], x[:, bass.ds(c * TB + t, 1), :]
                                           .rearrange("p a d -> p (a d)"))
                m.then_inc(s["stat_rows"], 1)
                dve.wait_ge(s["stat_rows"], k * 2 + 1)
                nc.vector.tensor_copy(pace[:, :], ident[:, 0:1])
                for t in range(TB):
                    m = nc.vector.bn_aggr(mean_var[:, t, :], bn[:, t, :])
                m.then_inc(s["stat_rows"], 1)
                dve.wait_ge(s["stat_rows"], k * 2 + 2)
                nc.vector.tensor_copy(mean[:, bass.ds(c * TB, TB)], mean_var[:, :, 0])
                nc.vector.tensor_scalar(var_eps[:, bass.ds(c * TB, TB)], mean_var[:, :, 1],
                                        EPS, None, ALU.add).then_inc(s["stat_bn"], 1)

            def normalise(c, done):
                for t in range(TB):
                    m = nc.vector.tensor_scalar(
                        xn[:, t, :], x[:, bass.ds(c * TB + t, 1), :].rearrange("p a d -> p (a d)"),
                        mean[:, bass.ds(c * TB + t, 1)], rstd[:, bass.ds(c * TB + t, 1)],
                        ALU.subtract, ALU.mult)
                m.then_inc(s[done], 1)

            def split_group_lo(k):
                c = slice(k * GT * P, (k + 1) * GT * P)
                for w, dst in enumerate((wg, wu, wd)):
                    dve.wait_ge(s["wsplit_hi"], k * 3 + w + 1)
                    nc.vector.tensor_tensor(dst[1][:, c], stage[:, k % 2, w, :], f32(dst[0][:, c]),
                                            ALU.subtract).then_inc(s["wsplit_lo"], 1)

            def step(ins):
                ins.then_inc(s["route"], 1)

            tt = nc.vector.tensor_tensor

            def route_scores(g):
                dve.wait_ge(s["sigmoid_done"], g + 1)
                step(tt(sc[:, :, :], score[:, :, :], bias[:, :].unsqueeze(1).broadcast_to([P, TB, E]),
                        ALU.add))
                dve.wait_ge(s["route"], g * ROUTE + 1)
                v = sc[:, :, :].rearrange("p t (a b) -> p (t a) b", a=G)
                step(tt(t4[0][:, :, :], v[:, :, 0:4], v[:, :, 4:8], ALU.max))
                step(tt(t4[1][:, :, :], v[:, :, 0:4], v[:, :, 4:8], ALU.min))

            def route_top2(g):
                hi, lo = t4
                dve.wait_ge(s["route"], g * ROUTE + 3)
                step(tt(t2[0][:, :, :], hi[:, :, 0:2], hi[:, :, 2:4], ALU.max))
                step(tt(t2[1][:, :, :], hi[:, :, 0:2], hi[:, :, 2:4], ALU.min))
                step(tt(t2[2][:, :, :], lo[:, :, 0:2], lo[:, :, 2:4], ALU.max))
                dve.wait_ge(s["route"], g * ROUTE + 6)
                step(tt(t2[3][:, :, :], t2[1][:, :, :], t2[2][:, :, :], ALU.max))

            def route_group_score(g):
                hi, lo = t2[0], t2[3]
                dve.wait_ge(s["route"], g * ROUTE + 7)
                step(tt(t1[0][:, :, :], hi[:, :, 0:1], hi[:, :, 1:2], ALU.max))
                step(tt(t1[1][:, :, :], hi[:, :, 0:1], hi[:, :, 1:2], ALU.min))
                step(tt(t1[2][:, :, :], lo[:, :, 0:1], lo[:, :, 1:2], ALU.max))
                dve.wait_ge(s["route"], g * ROUTE + 10)
                step(tt(t1[3][:, :, :], t1[1][:, :, :], t1[2][:, :, :], ALU.max))
                dve.wait_ge(s["route"], g * ROUTE + 11)
                step(tt(gscore[:, :, :], t1[0][:, :, :], t1[3][:, :, :], ALU.add))

            def route_group_rank(g):
                v = gscore[:, :, :].rearrange("p (t a) o -> p t (a o)", t=TB)
                other = v.unsqueeze(2).broadcast_to([P, TB, G, G])
                own = v.unsqueeze(3).broadcast_to([P, TB, G, G])
                dve.wait_ge(s["route"], g * ROUTE + 12)
                step(tt(gcmp[0][:, :, :, :], other, own, ALU.is_gt))
                step(tt(gcmp[1][:, :, :, :], other, own, ALU.is_equal))
                dve.wait_ge(s["route"], g * ROUTE + 14)
                step(tt(gcmp[2][:, :, :, :], gcmp[1][:, :, :, :], tie, ALU.mult))
                dve.wait_ge(s["route"], g * ROUTE + 15)
                step(tt(gcmp[1][:, :, :, :], gcmp[0][:, :, :, :], gcmp[2][:, :, :, :], ALU.add))

            def route_mask(g):
                dve.wait_ge(s["route"], g * ROUTE + 16)
                step(nc.vector.tensor_reduce(grank[:, :, 0], gcmp[1][:, :, :, :]
                                             .rearrange("p t a b -> p (t a) b"), AX.X, ALU.add))
                dve.wait_ge(s["route"], g * ROUTE + 17)
                step(nc.vector.tensor_scalar(gpen[:, :, :], grank[:, :, :], 1.5, NEG,
                                             ALU.is_gt, ALU.mult))
                dve.wait_ge(s["route"], g * ROUTE + 18)
                step(tt(masked[:, :, :].rearrange("p t (a b) -> p (t a) b", a=G),
                        sc[:, :, :].rearrange("p t (a b) -> p (t a) b", a=G),
                        gpen[:, :, :].broadcast_to([P, TB * G, EG]), ALU.add))

            def route_topk(g):
                dve.wait_ge(s["route"], g * ROUTE + 19)
                nc.vector.tensor_copy(pace[:, :], ident[:, 0:1])
                for t in range(TB):
                    step(nc.vector.max(top[:, t, :], masked[:, t, :]))

            def route_places(g):
                dve.wait_ge(s["route"], g * ROUTE + 23)
                nc.vector.tensor_copy(pace[:, :], ident[:, 0:1])
                for t in range(TB):
                    step(nc.vector.max_index(topi[:, t, :], top[:, t, :], masked[:, t, :]))
                dve.wait_ge(s["route"], g * ROUTE + 27)
                step(nc.vector.tensor_copy(topf[:, :, :], topi[:, :, :]))

            def route_onehot(g):
                dve.wait_ge(s["route"], g * ROUTE + 28)
                step(tt(onehot[:, :, :, :], iota.unsqueeze(1).broadcast_to([P, TB, E, TOPK]),
                        topf[:, :, 0:TOPK].unsqueeze(2).broadcast_to([P, TB, E, TOPK]),
                        ALU.is_equal))

            def route_chosen(g):
                dve.wait_ge(s["route"], g * ROUTE + 29)
                step(nc.vector.tensor_reduce(chosen[:, :, :], onehot[:, :, :, :], AX.X, ALU.add))
                step(tt(anch[:, :, :], onehot[:, :, 0:E:2, 0], onehot[:, :, 1:E:2, 0], ALU.add))

            def route_weights(g):
                dve.wait_ge(s["route"], g * ROUTE + 31)
                step(tt(wts[:, :, :], chosen[:, :, :], score[:, :, :], ALU.mult))
                step(nc.vector.tensor_scalar(cw[:, :, E:E + L], anch[:, :, :], 0.05, None, ALU.mult))
                dve.wait_ge(s["route"], g * ROUTE + 33)
                step(nc.vector.tensor_reduce(wsum[:, :, 0], wts[:, :, :], AX.X, ALU.add))
                dve.wait_ge(s["route"], g * ROUTE + 34)
                step(nc.vector.tensor_scalar(wsum_e[:, :, :], wsum[:, :, :], 1e-20, None, ALU.add))

            def route_scale(g):
                dve.wait_ge(s["route"], g * ROUTE + 35)
                step(nc.vector.reciprocal(wrec[:, :, :], wsum_e[:, :, :]))
                dve.wait_ge(s["route"], g * ROUTE + 36)
                step(nc.vector.tensor_scalar(wfac[:, :, :], wrec[:, :, :], 0.1, None, ALU.mult))
                dve.wait_ge(s["route"], g * ROUTE + 37)
                step(tt(cw[:, :, 0:E], wts[:, :, :], wfac[:, :, :].broadcast_to([P, TB, E]), ALU.mult))

            def route_parts(g, first):
                dve.wait_ge(s["route"], g * ROUTE + 38)
                if not first:
                    dve.wait_ge(s["cwT_ps"], g)
                step(nc.vector.tensor_copy(cw2[:, :, 0:ROWS].bitcast(F32R), cw[:, :, :]))
                dve.wait_ge(s["route"], g * ROUTE + 39)
                step(tt(cw2[:, :, ROWS:], cw[:, :, :], cw2[:, :, 0:ROWS], ALU.subtract))

            ROUTING = {7: route_scores, 8: route_top2, 9: route_group_score, 10: route_group_rank,
                       11: route_mask, 12: route_topk, 13: route_places, 14: route_onehot,
                       15: route_chosen, 16: route_weights, 17: route_scale}

            def xT_low(g):
                dve.wait_ge(s["xT_hi"], g + 1)
                tt(of_chunk(xT_parts[1], g), xT, f32(of_chunk(xT_parts[0], g)), ALU.subtract) \
                    .then_inc(s["xT_lo"], 1)

            def add_y(g, stats_before):
                c = g if stats_before is not None else g - NC
                xs = x[:, bass.ds(c * TB, TB), :]
                dve.wait_ge(s["yT_ps"], g + 1)
                tt(xs, xs, psM[:, :].rearrange("p (t d) -> p t d", t=TB), ALU.add) \
                    .then_inc(s["x_added"], 1)
                if stats_before is not None:
                    dve.wait_ge(s["x_added"], g + 1)
                    chunk_stats(c, c + stats_before)

            def ffn_chunk(g, g0, first, last, before):
                for j in range(HT):
                    if j == 0 and not last:
                        dve.wait_ge(s["xT_ps"], g + 1)
                        normalise(g + 1 - g0, "xn_ready")
                    dve.wait_ge(s["silu_done"], tiles(g, j))
                    if not (first and j < 3):
                        dve.wait_ge(s["z_lo"], tiles(g, j) - 3)
                    tt(z[j % 3], psU[j % 2][:, :], silu[j % 2], ALU.mult).then_inc(s["gated_done"], 1)
                    if j == 9 and not first:
                        add_y(g - 1, before)
                    if j == 5 and not last:
                        xT_low(g + 1)
                    if j in ROUTING and not last:
                        ROUTING[j](g + 1)
                    if j == 18 and not last:
                        route_parts(g + 1, False)
                    dve.wait_ge(s["gated_done"], tiles(g, j))
                    dve.wait_ge(s["spread_ps"], tiles(g, j))
                    tt(z[j % 3], z[j % 3], psW[j % 2][:, :], ALU.mult).then_inc(s["z_done"], 1)

            def ffn(g0, before):
                normalise(0, "xn_ready")
                for k in ROUTING:
                    ROUTING[k](g0)
                route_parts(g0, g0 == 0)
                xT_low(g0)
                ffn_chunk(g0, g0, True, False, before)
                with dve.Fori(g0 + 1, g0 + NC - 1) as g:
                    ffn_chunk(g, g0, False, False, before)
                ffn_chunk(g0 + NC - 1, g0, False, True, before)
                add_y(g0 + NC - 1, before)

            def a_rows(b, first):
                if not first:
                    dve.wait_ge(s["a_xT_ps"], b)
                    dve.wait_ge(s["a_xn_lo"], b)
                normalise(b, "a_xn")
                dve.wait_ge(s["a_xn"], b + 1)
                xs = x[:, bass.ds(b * TB, TB), :]
                tt(xs, xs, xn[:, :, :], ALU.add).then_inc(s["a_xres"], 1)

            def a_xT_low(b):
                dve.wait_ge(s["a_xT_hi"], b + 1)
                tt(of_chunk(xT_parts[1], b), psYh[:, :], f32(of_chunk(xT_parts[0], b)), ALU.subtract) \
                    .then_inc(s["a_xT_lo"], 1)

            def a_row_parts(b, first):
                if not first:
                    dve.wait_ge(s["ctx_ps"], b * H)
                nc.vector.tensor_copy(xnp[0][:, :, :], xn[:, :, :]).then_inc(s["a_xn_hi"], 1)
                dve.wait_ge(s["a_xn_hi"], b + 1)
                tt(xnp[1][:, :, :], xn[:, :, :], f32(xnp[0][:, :, :]), ALU.subtract) \
                    .then_inc(s["a_xn_lo"], 1)

            def y_lo(b, h):
                n = b * H + h
                dve.wait_ge(s["yh_hi"], n + 1)
                tt(yh[1][:, h % 2, :], psYh[:, :], f32(yh[0][:, h % 2, :]), ALU.subtract) \
                    .then_inc(s["yh_lo"], 1)

            def row_max(b, h, qb):
                n = b * H + h
                dve.wait_ge(s["s_ps"], n * 3 + (3, 3, 2, 1)[qb])
                nc.vector.tensor_reduce(nmax[:, h % 2, qb:qb + 1], scores_of(qb),
                                        AX.X, ALU.max, negate=True).then_inc(s["max_done"], 1)

            def pT_lo(b, h, part):
                n = b * H + h
                dve.wait_ge(s["pT_hi"], n * 3 + part + 1)
                o, w = ((0, 512), (640, 512), (1152, 256))[part]
                tt(pT[1][:, h % 2, o:o + w], psPT[part][:, 0:w], f32(pT[0][:, h % 2, o:o + w]),
                   ALU.subtract).then_inc(s["pT_lo"], 1)

            def row_rec(b, h, qb):
                n = b * H + h
                dve.wait_ge(s["exp_done"], n * TB + TB - qb)
                nc.vector.reciprocal(rrec[:, h % 2, qb:qb + 1], rsum[:, h % 2, qb:qb + 1]) \
                    .then_inc(s["rec_done"], 1)

            def add_out(b):
                dve.wait_ge(s["out_ps"], b * H + H)
                dve.wait_ge(s["a_xres"], b + 1)
                xs = x[:, bass.ds(b * TB, TB), :]
                tt(xs, xs, psO[:, :].rearrange("p (t d) -> p t d", t=TB), ALU.add) \
                    .then_inc(s["out_added"], 1)
                dve.wait_ge(s["out_added"], b + 1)
                chunk_stats(b, b + 2 * NC)

            def attn_slot(b, sl, first, last):
                nxt = lambda k: (b, sl + k) if sl + k < H else (b + 1, sl + k - H)
                have_y = not (last and sl + 2 >= H)
                have_s = not (last and sl + 1 >= H)
                if have_s:
                    for qb in (3, 2, 1, 0):
                        row_max(*nxt(1), qb)
                if sl == 2 and not first:
                    add_out(b - 1)
                if sl == 6 and not last:
                    a_rows(b + 1, False)
                if sl == 0 and not first:
                    a_row_parts(b, False)
                if have_s:
                    for qb in (3, 2, 1, 0):
                        row_rec(*nxt(1), qb)
                if have_y:
                    y_lo(*nxt(2))
                pT_lo(b, sl, 0)
                pT_lo(b, sl, 1)
                if sl == 8 and not last:
                    a_xT_low(b + 1)
                pT_lo(b, sl, 2)

            def attention():
                for k in range(H // TB):
                    dve.wait_ge(s["mb_hi"], k + 1)
                    nc.vector.scalar_tensor_tensor(
                        out=head_columns(mh[1], k),
                        in0=psG[k % 2][:, :].rearrange("p (j d) -> p j d", d=P),
                        scalar=float(DK) ** -0.5, in1=f32(head_columns(mh[0], k)),
                        op0=ALU.mult, op1=ALU.subtract).then_inc(s["mb_lo"], 1)
                dve.wait_ge(s["down_ps"], NC * HT)
                for t in pT:
                    m = nc.vector.memset(t[:, :, 512:640].bitcast(F32), 0.0)
                m.then_inc(s["zeroed"], 1)
                finish_std(2)
                a_rows(0, True)
                a_xT_low(0)
                a_row_parts(0, True)
                y_lo(0, 0)
                for qb in (3, 2, 1, 0):
                    row_max(0, 0, qb)
                for qb in (3, 2, 1, 0):
                    row_rec(0, 0, qb)
                y_lo(0, 1)
                for sl in range(H):
                    attn_slot(0, sl, True, False)
                with dve.Fori(1, NC - 1) as b:
                    for sl in range(H):
                        attn_slot(b, sl, False, False)
                for sl in range(H):
                    attn_slot(NC - 1, sl, False, True)
                add_out(NC - 1)

            dve.wait_ge(s["consts_loaded"], 48)
            for c in range(NC):
                dve.wait_ge(x_loads[c], 16)
                chunk_stats(c, c)
            nc.vector.tensor_copy(half[:, :], small[:, 0:2 * P])
            nc.vector.memset(cw[:, :, E + L + 1:], 0.0)
            nc.vector.memset(cw[:, :, E + L:E + L + 1], 0.5).then_inc(s["cw_const"], 1)
            dve.wait_ge(s["cw_const"], 1)
            finish_std(1)
            for k in range(CONV_GROUPS):
                split_group_lo(k)
            ffn(0, NC)
            attention()
            finish_std(3)
            ffn(NC, None)

        @block.gpsimd
        def _(pool):
            pool.dma_start(sel[:, :], sel_in).then_inc(s["sel_loaded"], 16)
            pool.wait_ge(s["consts_loaded"], 48)

            def z_low(g, j):
                pool.wait_ge(s["z_hi"], tiles(g, j))
                nc.gpsimd.tensor_tensor(zp[1][part_slot(j)], z[j % 3], f32(zp[0][part_slot(j)]),
                                        ALU.subtract).then_inc(s["z_lo"], 1)

            def norm(n, par):
                for qb in (3, 2, 1, 0):
                    pool.wait_ge(s["rec_done"], (2 * n + par) * TB + TB - qb)
                    k = par * TB + qb
                    nc.gpsimd.tensor_tensor(pool_pace[:, k:k + 1], ident[:, 0:1], ident[:, 0:1], ALU.add)
                    o = qb * (qb + 1) // 2 * P
                    p = prob[:, par, o:o + (qb + 1) * P]
                    nc.gpsimd.tensor_scalar(p, p, rrec[:, par, qb:qb + 1], 1.0, ALU.mult, ALU.mult) \
                        .then_inc(s["norm_done"], 1)

            with pool.Fori(0, NC) as g:
                for j in range(HT):
                    z_low(g, j)
            with pool.Fori(0, NC * H // 2) as n:
                norm(n, 0)
                norm(n, 1)
            with pool.Fori(NC, 2 * NC) as g:
                for j in range(HT):
                    z_low(g, j)


def kernel(L0_attn_x, L0_attn_Wq, L0_attn_Wk, L0_attn_Wv, L0_attn_Wo, L0_ffn_gate_weight,
           L0_ffn_gate_bias, L0_ffn_w_gate, L0_ffn_w_up, L0_ffn_w_down, L0_ffn_shared_w_gate,
           L0_ffn_shared_w_up, L0_ffn_shared_w_down, L0_ffn_anchor_w_gate, L0_ffn_anchor_w_up,
           L0_ffn_anchor_w_down):
    import concourse.bacc as bacc
    from concourse.bass_utils import run_bass_kernel_spmd

    x = np.asarray(L0_attn_x)
    B, S, D = x.shape

    def hidden_columns(experts, anchors, shared):
        parts = [np.asarray(w).transpose(1, 0, 2).reshape(D, -1) for w in (experts, anchors)]
        parts.append(np.asarray(shared))
        w = np.zeros((D, HT * P), np.float32)
        w[:, :sum(p.shape[1] for p in parts)] = np.concatenate(parts, 1)
        return w

    down = np.zeros((HT * P, D), np.float32)
    rows = np.concatenate([np.asarray(L0_ffn_w_down).reshape(-1, D),
                           np.asarray(L0_ffn_anchor_w_down).reshape(-1, D),
                           np.asarray(L0_ffn_shared_w_down)], 0)
    down[:rows.shape[0]] = rows
    small, sel = constants()
    arrays = {
        "x": x.reshape(B * S, D),
        "w_gate": hidden_columns(L0_ffn_w_gate, L0_ffn_anchor_w_gate, L0_ffn_shared_w_gate),
        "w_up": hidden_columns(L0_ffn_w_up, L0_ffn_anchor_w_up, L0_ffn_shared_w_up),
        "w_down": down.reshape(HT, P, D).transpose(1, 0, 2).reshape(P, HT * D),
        "gate_weight": np.asarray(L0_ffn_gate_weight).T,
        "gate_bias": np.asarray(L0_ffn_gate_bias),
        "wqT": np.asarray(L0_attn_Wq).T,
        "wkT": np.asarray(L0_attn_Wk).T,
        "wvT": np.asarray(L0_attn_Wv).T,
        "wo": np.asarray(L0_attn_Wo),
        "small": small, "sel": sel,
    }
    arrays = {n: np.ascontiguousarray(a) for n, a in arrays.items()}
    nc = bacc.Bacc("TRN2", target_bir_lowering=False, num_devices=1)
    args = [nc.dram_tensor("in_" + n, a.shape, mybir.dt.from_np(a.dtype), kind="ExternalInput").ap()
            for n, a in arrays.items()]
    out = nc.dram_tensor("out_rows", (B * S, D), F32, kind="ExternalOutput").ap()
    build(nc, *args, out)
    r = run_bass_kernel_spmd(nc, [{"in_" + n: a for n, a in arrays.items()}], core_ids=[0])
    return r.results[0]["out_rows"].reshape(B, S, D)
```

```python
from contextlib import ExitStack

import numpy as np

import concourse.bass as bass
from concourse import mybir

ALU = mybir.AluOpType
ACT = mybir.ActivationFunctionType
AX = mybir.AxisListType
F32 = mybir.dt.float32
F32R = mybir.dt.float32r
BF16 = mybir.dt.bfloat16
U32 = mybir.dt.uint32

P = 128
TB = 4
CH = TB * P
E, G, TOPK, MI = 32, 4, 6, 64
EG = E // G
L, AI = 16, 32
ROWS = E + L
NSPREAD = 4
SPREAD_TILES = (E * MI + L * AI) // P
HT = (E * MI + L * AI + MI + P - 1) // P
H, DK = 16, 64
LAG = 3
NEG = -1.0e30
EPS = 1e-5
KB_OFF = [0, 4 * P, 7 * P]
PT_W = 10 * P
PT_PARTS = [(0, 0, 4 * P), (P, 4 * P, 3 * P), (0, 7 * P, 2 * P)]
MB = 2 * H // TB
PW = TB * (TB + 1) // 2 * P
W_GROUPS = 3
GT = HT // W_GROUPS


def constants():
    ident = np.eye(P, dtype=np.float32)
    mask = np.where(np.arange(P)[None, :] > np.arange(P)[:, None], NEG, 0.0)
    iota = np.broadcast_to(np.arange(E, dtype=np.float32)[None, :, None], (P, E, TOPK))
    tie = np.broadcast_to((np.arange(G)[None, :] < np.arange(G)[:, None]), (P, TB, G, G))
    small = np.concatenate([ident, mask, iota.reshape(P, -1), tie.reshape(P, -1)], 1)
    return small.astype(np.float32)


def build(nc, x_in, wg_in, wu_in, wd_in, gate_in, bias_in, wqT_in, wkT_in, wvT_in, wo_in,
          small_in, cw_rows, out):
    T = x_in.shape[0]
    NT = T // P
    NC = T // CH
    HC = HT * P
    ctx = ExitStack()
    with ctx:
        def sb(name, shape, dt=F32):
            return ctx.enter_context(nc.sbuf_tensor(name, shape, dt))

        def sb_shared(name, shape, dt=F32):
            with nc.sbuf_tensor(name, shape, dt) as t:
                return t

        def sem(name):
            return ctx.enter_context(nc.semaphore(name))

        small = sb("small", [P, 2 * P + E * TOPK + TB * G * G])
        ident = small[:, 0:P]
        iota = small[:, 2 * P:2 * P + E * TOPK].rearrange("p (e k) -> p e k", e=E)
        tie = small[:, 2 * P + E * TOPK:].rearrange("p (t a b) -> p t a b", t=TB, a=G)
        half = sb("half", [P, 3 * P], BF16)
        ident_bf, mask_bf = half[:, 0:P], half[:, P:3 * P]
        gate_w = sb("gate_w", [P, E])
        bias = sb("bias", [P, E])
        wg = [sb(f"wg_{n}", [P, HC], F32R) for n in ("hi", "lo")]
        wu = [sb(f"wu_{n}", [P, HC], F32R) for n in ("hi", "lo")]
        wd = [sb(f"wd_{n}", [P, HC], F32R) for n in ("hi", "lo")]
        stage = sb("stage", [P, 2, 3, GT * P])
        attn_w = stage[:, :, :, :].rearrange("p a b c -> p (a b c)")[:, 0:4 * H * DK] \
            .rearrange("p (w j d) -> p w j d", w=4, j=H // 2)
        spare = stage[:, :, :, :].rearrange("p a b c -> p (a b c)")[:, 4 * H * DK:]
        key0 = spare[:, 0:2 * P]
        rows3 = spare[:, 2 * P:3 * P]
        xT_first = spare[:, 3 * P:3 * P + CH]
        outT = xT_first
        b_whole = stage[:, :, :, :].rearrange("p a b c -> p (a b c)")[:, 0:H * P]
        mh = [sb(f"m_{n}", [P, H * P], F32R) for n in ("hi", "lo")]
        spread = sb_shared("spread", [P, NSPREAD, CH])
        bh_lo = sb("b_lo", [P, H * P], F32R)
        bh = [sb("b_hi", [P, H * P], F32R), bh_lo]
        x = sb("x", [P, NT, P])
        bn = sb("bn", [P, TB, 6])
        mean_var = sb("mean_var", [P, TB, 2])
        mean = sb("mean", [P, NT])
        var_eps = sb("var_eps", [P, NT])
        std = sb("std", [P, NT])
        rstd0 = sb("rstd0", [P, NT])
        newton = sb("newton", [P, NT])
        pool_pace = sb("pool_pace", [P, 2 * TB])
        pace = sb("pace", [P, 1])
        rstd = sb("rstd", [P, NT])
        xn = sb("xn", [P, TB, P])
        xT_parts = [sb(f"xT_{n}", [P, 2 * CH], F32R) for n in ("hi", "lo")]
        score = sb("score", [P, TB, E])
        sc = sb("sc", [P, TB, E])
        t4 = [sb(f"t4_{i}", [P, TB * G, 4]) for i in range(2)]
        t2 = [sb(f"t2_{i}", [P, TB * G, 2]) for i in range(4)]
        t1 = [sb(f"t1_{i}", [P, TB * G, 1]) for i in range(4)]
        gscore = sb("gscore", [P, TB * G, 1])
        gcmp = [sb(f"gcmp_{i}", [P, TB, G, G]) for i in range(3)]
        grank = sb("grank", [P, TB * G, 1])
        gpen = sb("gpen", [P, TB * G, 1])
        masked = sb("masked", [P, TB, E])
        top = sb("top", [P, TB, 8])
        topi = sb("topi", [P, TB, 8], U32)
        topf = sb("topf", [P, TB, 8])
        onehot = sb("onehot", [P, TB, E, TOPK])
        chosen = sb("chosen", [P, TB, E])
        wts = sb("wts", [P, TB, E])
        wsum = sb("wsum", [P, TB, 1])
        wsum_e = sb("wsum_e", [P, TB, 1])
        wrec = sb("wrec", [P, TB, 1])
        anch = sb("anch", [P, TB, L])
        cw = sb("cw", [P, TB, P])
        cwT = sb("cwT", [ROWS, CH])
        prob = sb("prob", [P, 2, PW])
        pT = [sb(f"pT_{n}", [P, 2, PT_W], F32R) for n in ("hi", "lo")]
        pT3 = sb("pT_3", [P, 2, P])
        yh = [sb(f"y_{n}", [P, 2, CH - P], F32R) for n in ("hi", "lo")]
        yh0 = sb("y_0", [P, 2, P])
        row_parts = sb("row_parts", [P, 2, TB, P], F32R)
        xnp = [row_parts[:, i, :, :] for i in (0, 1)]
        ffn_T = sb_shared("ffn_T", [P, 2, CH])
        ctx_hi = sb("ctx_hi", [P, 2, CH], F32R)
        ctx_lo = sb("ctx_lo", [P, CH], F32R)
        yT, xT = ffn_T[:, 0, :], ffn_T[:, 1, :]
        nmax = sb("nmax", [P, 2, TB])
        rsum = sb("rsum", [P, 2, TB])
        rrec = sb("rrec", [P, 2, TB])
        ffn_f = prob[:, :, :].rearrange("p a b -> p (a b)")
        silu = [ffn_f[:, i * CH:(i + 1) * CH] for i in (0, 1)]
        z = [ffn_f[:, i * CH:(i + 1) * CH] for i in (2, 3, 4)]
        NZ = 5
        pT_flat = [t[:, :, :].rearrange("p a b -> p (a b)") for t in pT]
        zp = [[t[:, i * CH:(i + 1) * CH] for i in range(NZ)] for t in pT_flat]

        bank = [ctx.enter_context(nc.psum_tensor(f"bank{i}", [P, 512], F32)) for i in range(8)]
        psG, psU, psY, psM = bank[0:3], bank[3:6], bank[6], bank[7]
        psS, psPT, psYh, psC, psO = bank[0:3], [bank[3], bank[4], bank[3]], bank[5], bank[6], bank[7]
        psS_u = (2, 2, 1, 0)

        names = """consts_loaded attn_w_loaded
            stat_dve stat_act stat_rows stat_bn
            xn_ready xT_ps xT_sb logits_ps sigmoid_done route cwT_ps cwT_sb xT_hi xT_lo
            gate_up_ps cw_stored silu_done gated_done z_done z_hi z_lo down_ps
            y_evac yT_ps x_added
            mb_ps mb_hi mb_lo
            a_xn key0_sb rows3_sb a_xT_ps a_xT_hi a_xT_lo a_xres a_xn_hi a_xn_lo
            yh_ps yh_whole yh_hi yh_lo s_ps max_done exp_done rec_done norm_done
            pT_ps pT_whole pT_hi pT_lo b_lo ctx_ps ctx_hi ctx_lo out_ps outT_sb outT_ps out_added stored""".split()
        s = {n: sem("s_" + n) for n in names}
        x_loads = [sem(f"s_x_load{c}") for c in range(NC)]
        w_loads = [sem(f"s_w_load{k}") for k in range(W_GROUPS)]

        spread_loads = [sem(f"s_spread{k}") for k in range(NSPREAD)]
        wsplit_hi = [sem(f"s_wsplit_hi{k}") for k in range(W_GROUPS)]
        wsplit = [sem(f"s_wsplit{k}") for k in range(W_GROUPS)]

        block = ctx.enter_context(nc.Block())

        def f32(ap):
            return ap.bitcast(F32)

        def mm3(pe, o, w, m, start, stop):
            pe.matmul(o, w[0], m[0], start=start, stop=False, skip_group_check=True)
            pe.matmul(o, w[0], m[1], start=False, stop=False, skip_group_check=True)
            return pe.matmul(o, w[1], m[0], start=False, stop=stop, skip_group_check=True)

        def of_chunk(ring, c, o=0, w=CH):
            if isinstance(c, int):
                return ring[:, (c % 2) * CH + o:(c % 2) * CH + o + w]
            return ring[:, bass.ds((c % 2) * CH + o, w)]

        def tiles(g, j):
            return g * HT + j + 1

        def two_ago(g, j):
            return g * HT + (j - 1 if j > 1 else -j)

        def spread_count(g, j):
            return 16 * (g * (SPREAD_TILES // NSPREAD) + j // NSPREAD + 1)

        def part_slot(j):
            return j % 4 if j < HT - 1 else 4

        def part_slot_free(g, j):
            return tiles(g, j) - (HT if j == HT - 1 else 4 if j > 3 else 5)

        ROUTE = 37

        def weight_heads(k):
            k %= H // TB
            return [(k // 2) * 2 * TB + 2 * i + k % 2 for i in range(TB)]

        def head_columns(t, k):
            h = weight_heads(k)[0]
            return t[:, :].rearrange("p (j two d) -> p j two d", two=2, d=P)[:, h // 2:h // 2 + TB, h % 2, :]

        def scores_of(qb):
            o = 2 * P if qb == 0 else 0
            return psS[psS_u[qb]][:, o:o + (qb + 1) * P]

        def key0_of(b):
            if isinstance(b, int):
                return key0[:, (b % 2) * P:(b % 2 + 1) * P]
            return key0[:, bass.ds((b % 2) * P, P)]

        STD = [(0, 1, 1), (1, 2, 2), (2, NC, NC), (0, NC - 1, 2 * NC - 1), (NC - 1, NC, 2 * NC),
               (0, NC - 1, 3 * NC - 1), (NC - 1, NC, 3 * NC)]

        XT, LOGITS, YT, CWT = 2, 5, 8, 18
        SPLIT_LAST = (1, 2, 3), (5, 7, 9)
        MB_SLOT = 10

        @block.sync
        def _(sp):
            def load_group(sp, k):
                cols = slice(k * GT * P, (k + 1) * GT * P)
                for w, src in enumerate((wg_in, wu_in, wd_in)):
                    sp.dma_start(stage[:, k % 2, w, :], src[:, cols]).then_inc(w_loads[k], 16)

            def load_x(sp, c):
                sp.dma_start(x[:, c * TB:(c + 1) * TB, :],
                             x_in[c * CH:(c + 1) * CH, :].rearrange("(t p) d -> p t d", p=P)) \
                    .then_inc(x_loads[c], 16)

            sp.dma_start(small[:, :], small_in).then_inc(s["consts_loaded"], 16)
            load_x(sp, 0)
            sp.dma_start(gate_w[:, :], gate_in).then_inc(s["consts_loaded"], 16)
            sp.dma_start(bias[:, :], bias_in.partition_broadcast(P)).then_inc(s["consts_loaded"], 16)
            load_group(sp, 0)
            load_x(sp, 1)
            load_group(sp, 1)
            for c in range(2, NC):
                load_x(sp, c)
            for k in range(2, W_GROUPS):
                sp.wait_ge(wsplit[k - 2], 3)
                load_group(sp, k)

            def spread_weights(g, first, store=None, after_attention=False):
                sp.wait_ge(s["cwT_sb"], g + 1)
                rows = cw_rows[bass.ds((g % 2) * ROWS, ROWS), :] if not isinstance(g, int) else \
                    cw_rows[(g % 2) * ROWS:(g % 2 + 1) * ROWS, :]
                sp.dma_start(rows, cwT[:, :]).then_inc(s["cw_stored"], 16)
                sp.wait_ge(s["cw_stored"], 16 * (g + 1))
                if after_attention:
                    sp.wait_ge(s["out_ps"], NC * H)
                for j in range(SPREAD_TILES):
                    if not (first and j < NSPREAD):
                        sp.wait_ge(s["z_done"], g * HT + j + 1 - NSPREAD - (1 if j < NSPREAD else 0))
                    n = P // (MI if j < E * MI // P else AI)
                    row = j * 2 if j < E * MI // P else E + (j - E * MI // P) * n
                    row = (g % 2) * ROWS + row
                    src = cw_rows[row:row + n, :] if isinstance(g, int) else \
                        cw_rows[bass.ds(row, n), :]
                    sp.dma_start(spread[:, j % NSPREAD, :],
                                 src.unsqueeze(1).broadcast_to([n, P // n, CH])) \
                        .then_inc(spread_loads[j % NSPREAD], 16)
                    if j == 11 and store is not None:
                        store_chunk(store)

            def store_chunk(c):
                sp.wait_ge(s["x_added"], (c + NC) + 1)
                sp.dma_start(out[bass.ds(c * CH, CH), :].rearrange("(t p) d -> p t d", p=P),
                             x[:, bass.ds(c * TB, TB), :]).then_inc(s["stored"], 16)

            spread_weights(0, True)
            for k in range(W_GROUPS):
                sp.wait_ge(wsplit[k], 3)
            for w, src in enumerate((wqT_in, wkT_in, wvT_in, wo_in)):
                sp.dma_start(attn_w[:, w, :, :], src.rearrange("(j p) d -> p j d", p=P)) \
                    .then_inc(s["attn_w_loaded"], 16)
            with sp.Fori(1, NC) as g:
                spread_weights(g, False)
            spread_weights(NC, False, after_attention=True)
            with sp.Fori(NC + 1, 2 * NC) as g:
                spread_weights(g, False, g - 1 - NC)
            store_chunk(NC - 1)
            sp.wait_ge(s["stored"], 16 * NC)

        @block.tensor
        def _(pe):
            def to_columns(dst, src, n=TB):
                for t in range(n):
                    m = pe.transpose(dst[:, t * P:(t + 1) * P], src[:, t, :], ident)
                return m

            def prep_xT(g):
                pe.wait_ge(s["xn_ready"], g + 1)
                to_columns(psM, xn).then_inc(s["xT_ps"], 1)

            def logits(g, ps, xT):
                pe.wait_ge(s["xT_hi"], g + 1)
                for t in range(TB):
                    m = pe.matmul(ps[:, t * E:(t + 1) * E], xT[:, t * P:(t + 1) * P], gate_w[:, :],
                                  start=True, stop=True, skip_group_check=True)
                m.then_inc(s["logits_ps"], 1)

            def prep_logits(g):
                logits(g, psM, xT)

            def prep_cwT(g, ps=psM):
                pe.wait_ge(s["route"], (g + 1) * ROUTE)
                to_columns(ps, cw).then_inc(s["cwT_ps"], 1)

            def gate_up(g, j, first):
                if j == 0:
                    pe.wait_ge(s["xT_lo"], g + 1)
                if not (first and j < 3):
                    pe.wait_ge(s["gated_done"], tiles(g, j) - 3)
                c = slice(j * P, (j + 1) * P)
                xp = [of_chunk(t, g) for t in xT_parts]
                mm3(pe, psG[j % 3][:, :], [w[:, c] for w in wg], xp, True, True)
                mm3(pe, psU[j % 3][:, :], [w[:, c] for w in wu], xp, True, True) \
                    .then_inc(s["gate_up_ps"], 1)

            def down(g, j, first):
                pe.wait_ge(s["z_lo"], tiles(g, j))
                if j == 0 and not first:
                    pe.wait_ge(s["y_evac"], g)
                c = slice(j * P, (j + 1) * P)
                mm3(pe, psY[:, :], [w[:, c] for w in wd], [zp[0][part_slot(j)], zp[1][part_slot(j)]],
                    j == 0, j == HT - 1).then_inc(s["down_ps"], 1)

            def post_yT(g):
                pe.wait_ge(s["y_evac"], g + 1)
                to_columns(psM, yT.rearrange("p (t d) -> p t d", t=TB)).then_inc(s["yT_ps"], 1)

            def ffn_chunk(g, first, last, setup=False, mb=False):
                for j in range(HT):
                    if setup and j % GT == 0:
                        pe.wait_ge(wsplit[j // GT], 3)
                    if j == XT and not last:
                        if first and g == NC:
                            pe.wait_ge(s["out_added"], NC)
                        prep_xT(g + 1)
                    if j == 2 and first and g == NC:
                        pe.wait_ge(s["cwT_sb"], NC + 1)
                    if j == LOGITS and not last:
                        prep_logits(g + 1)
                    if j == YT and not first:
                        if not last:
                            pe.wait_ge(s["sigmoid_done"], g + 2)
                        post_yT(g - 1)
                    gate_up(g, j, first)
                    if mb and j >= MB_SLOT and j - MB_SLOT < MB:
                        attn_products(j - MB_SLOT)
                    if mb and j == HT - 2:
                        pe.wait_ge(s["mb_hi"], MB)
                        a_prep(0, psM)
                    if j >= LAG:
                        down(g, j - LAG, first)
                    elif not first:
                        down(g - 1, HT - LAG + j, False)
                    if j == CWT and not last:
                        if not first:
                            pe.wait_ge(s["x_added"], g)
                        prep_cwT(g + 1)

            def ffn(g0):
                if g0 == 0:
                    prep_xT(g0)
                    prep_logits(g0)
                    prep_cwT(g0)
                ffn_chunk(g0, True, False, setup=g0 == 0)
                with pe.Fori(g0 + 1, g0 + NC - 1) as g:
                    ffn_chunk(g, False, False)
                ffn_chunk(g0 + NC - 1, False, True, mb=g0 == 0)
                down(g0 + NC - 1, HT - 3, False)
                down(g0 + NC - 1, HT - 2, False)
                if g0 == 0:
                    pe.wait_ge(s["gated_done"], tiles(NC - 1, HT - 1))
                    head_y(0, 0)
                down(g0 + NC - 1, HT - 1, False)
                if g0 == 0:
                    for u in range(3):
                        head_scores(0, 0, u, True)
                pe.wait_ge(s["x_added"], g0 + NC - 1)
                if g0 == 0:
                    pe.wait_ge(s["a_xT_lo"], 1)
                post_yT(g0 + NC - 1)

            def attn_products(k):
                if k == 0:
                    pe.wait_ge(s["attn_w_loaded"], 64)
                    pe.wait_ge(s["x_added"], NC - 1)
                else:
                    pe.wait_ge(s["mb_hi"], k)
                    pe.wait_ge(s["mb_lo"], min(k, H // TB))
                for i, h in enumerate(weight_heads(k)):
                    r = slice((h % 2) * DK, (h % 2) * DK + DK)
                    a, c = (0, 1) if k < H // TB else (2, 3)
                    m = pe.matmul(psM[:, i * P:(i + 1) * P], attn_w[r, a, h // 2, :],
                                  attn_w[r, c, h // 2, :], start=True, stop=True,
                                  skip_group_check=True)
                m.then_inc(s["mb_ps"], 1)

            def a_prep(b, ps):
                pe.wait_ge(s["a_xn"], b + 1)
                to_columns(ps, xn).then_inc(s["a_xT_ps"], 1)

            def head_y(b, h):
                n = b * H + h
                if h == 0:
                    pe.wait_ge(s["a_xT_lo"], b + 1)
                if not (isinstance(b, int) and n == 0):
                    pe.wait_ge(s["yh_lo"], n)
                c = slice(h * P, (h + 1) * P)
                mm3(pe, psYh[:, :], [w[:, c] for w in mh], [of_chunk(t, b) for t in xT_parts],
                    True, True).then_inc(s["yh_ps"], 1)

            def head_scores(b, h, u, first):
                n = b * H + h
                if u == 0:
                    pe.wait_ge(s["yh_lo"], n + 1)
                if not (first and h == 0):
                    pe.wait_ge(s["exp_done"], (n - 1) * TB + (1, 2, 4)[u])
                qb = (3, 2, 1)[u]
                w = (qb + 1) * P
                q = slice((qb - 1) * P, qb * P)
                mm3(pe, psS[u][:, 0:w], [t[:, h % 2, q] for t in yh],
                    [of_chunk(t, b, 0, w) for t in xT_parts], True, False)
                if u == 2:
                    pe.matmul(psS[u][:, w:w + P], yh0[:, h % 2, :], key0_of(b),
                              start=False, stop=False, skip_group_check=True)
                m = pe.matmul(psS[u][:, qb * P:w + (P if u == 2 else 0)], ident_bf,
                              mask_bf[:, 0:(2 if u == 2 else 1) * P],
                              start=False, stop=True, skip_group_check=True)
                m.then_inc(s["s_ps"], 1)

            def head_probT(b, h, part, first):
                n = b * H + h
                if part == 0:
                    pe.wait_ge(s["norm_done"], n * TB + TB)
                if part == 2:
                    pe.wait_ge(s["pT_lo"], n * 3 + 1)
                elif not (first and h == 0):
                    pe.wait_ge(s["pT_lo"], (n - 1) * 3 + (3 if part == 0 else 2))
                blocks = [[(0, q) for q in range(TB)],
                          [(3, 3)] + [(1, q) for q in range(1, TB)],
                          [(2, q) for q in range(2, TB)]][part]
                for i, (kb, q) in enumerate(blocks):
                    o = q * (q + 1) // 2 * P + kb * P
                    m = pe.transpose(psPT[part][:, i * P:(i + 1) * P], prob[:, h % 2, o:o + P], ident)
                m.then_inc(s["pT_ps"], 1)

            def head_pv(b, h, kb, first):
                n = b * H + h
                if kb == 0:
                    pe.wait_ge(s["pT_lo"], n * 3 + 3)
                    if h == 0:
                        pe.wait_ge(s["a_xn_lo"], b + 1)
                    if not (first and h == 0):
                        pe.wait_ge(s["ctx_lo"], n)
                if kb < 3:
                    o, w = KB_OFF[kb], (TB - kb) * P
                    mm3(pe, psC[:, kb * P:CH], [t[:, kb, :] for t in xnp],
                        [t[:, h % 2, o:o + w] for t in pT], kb == 0, False)
                else:
                    pe.matmul(psC[:, kb * P:CH], rows3, pT3[:, h % 2, :], start=False,
                              stop=True, skip_group_check=True).then_inc(s["ctx_ps"], 1)

            def head_out(b, h, first):
                n = b * H + h
                pe.wait_ge(s["ctx_lo"], n + 1)
                if h == 0 and not first:
                    pe.wait_ge(s["out_added"], b)
                if h == 0 and first:
                    pe.wait_ge(s["x_added"], NC)
                    pe.wait_ge(s["b_lo"], H // TB)
                mm3(pe, psO[:, :], [t[:, h * P:(h + 1) * P] for t in bh],
                    [ctx_hi[:, h % 2, :], ctx_lo[:, :]], h == 0, h == H - 1).then_inc(s["out_ps"], 1)

            def rows_out(b):
                pe.wait_ge(s["outT_sb"], b + 1)
                to_columns(psO, outT.rearrange("p (t d) -> p t d", t=TB)).then_inc(s["outT_ps"], 1)

            def attn_slot(b, sl, first, last):
                nxt = lambda k: (b, sl + k) if sl + k < H else (b + 1, sl + k - H)
                prv = lambda k: (b, sl - k) if sl >= k else (b - 1, sl - k + H)
                have_y = not (last and sl + 2 >= H)
                have_s = not (last and sl + 1 >= H)
                have_v = not (first and sl < 1)
                have_o = not (first and sl < 2)
                if have_s:
                    for u in range(3):
                        head_scores(*nxt(1), u, False)
                head_probT(b, sl, 0, first)
                head_probT(b, sl, 1, first)
                if sl == 2 and not first:
                    rows_out(b - 1)
                if sl == 9 and not last:
                    pe.wait_ge(s["a_xT_lo"], b + 2)
                if sl == 9 and last:
                    pe.wait_ge(s["xT_lo"], NC + 1)
                if sl == 10 and last:
                    pe.wait_ge(s["sigmoid_done"], NC + 1)
                if have_y:
                    head_y(*nxt(2))
                if have_v:
                    for kb in range(TB):
                        head_pv(*prv(1), kb, first and sl < 2)
                if have_o:
                    head_out(*prv(2), first and sl - 2 < H)
                head_probT(b, sl, 2, first)
                if sl == 8 and not last:
                    pe.wait_ge(s["yh_lo"], b * H + 11)
                    a_prep(b + 1, psYh)
                if last and sl == 8:
                    pe.wait_ge(s["yh_lo"], b * H + 11)
                    pe.wait_ge(s["xn_ready"], NC + 1)
                    to_columns(psYh, xn).then_inc(s["xT_ps"], 1)
                if last and sl == 9:
                    pe.wait_ge(s["yh_lo"], b * H + 12)
                    logits(NC, psYh, xT_first)

            def attention():
                head_y(0, 1)
                for sl in range(H):
                    attn_slot(0, sl, True, False)
                with pe.Fori(1, NC - 1) as b:
                    for sl in range(H):
                        attn_slot(b, sl, False, False)
                for sl in range(H):
                    attn_slot(NC - 1, sl, False, True)
                prep_cwT(NC, psYh)
                head_out(NC - 1, H - 2, False)
                for kb in range(TB):
                    head_pv(NC - 1, H - 1, kb, False)
                head_out(NC - 1, H - 1, False)
                rows_out(NC - 1)

            ffn(0)
            attention()
            ffn(NC)

        @block.scalar
        def _(act):
            def row_std(n):
                c0, c1, measured = STD[n]
                act.wait_ge(s["stat_bn"], measured)
                c = slice(c0 * TB, c1 * TB)
                nc.scalar.activation(std[:, c], var_eps[:, c], ACT.Sqrt).then_inc(s["stat_act"], 1)

            def prep_copy(g, ps=psM, whole=xT):
                act.wait_ge(s["xT_ps"], g + 1)
                nc.scalar.activation(whole, ps[:, :], ACT.Copy).then_inc(s["xT_sb"], 1)
                nc.scalar.activation(of_chunk(xT_parts[0], g), ps[:, :], ACT.Copy) \
                    .then_inc(s["xT_hi"], 1)

            def prep_sigmoid(g, first=False, ps=psM):
                act.wait_ge(s["logits_ps"], g + 1)
                if not first:
                    act.wait_ge(s["route"], g * ROUTE)
                nc.scalar.activation(score[:, :, :].rearrange("p t e -> p (t e)"), ps[:, 0:TB * E],
                                     ACT.Sigmoid).then_inc(s["sigmoid_done"], 1)

            def prep_cwT(g, ps=psM):
                act.wait_ge(s["cwT_ps"], g + 1)
                if not (isinstance(g, int) and g == 0):
                    act.wait_ge(s["cw_stored"], 16 * g)
                nc.scalar.activation(cwT[:, :], ps[0:ROWS, :], ACT.Copy).then_inc(s["cwT_sb"], 1)

            def z_hi(g, j, early):
                act.wait_ge(s["z_done"], tiles(g, j))
                if not early:
                    act.wait_ge(s["down_ps"], part_slot_free(g, j))
                nc.scalar.activation(zp[0][part_slot(j)], z[j % 3], ACT.Copy).then_inc(s["z_hi"], 1)

            def y_copy(g):
                act.wait_ge(s["down_ps"], tiles(g, HT - 1))
                nc.scalar.activation(yT, psY[:, :], ACT.Copy).then_inc(s["y_evac"], 1)

            def split_hi(k, ws=range(3)):
                act.wait_ge(w_loads[k], 48)
                c = slice(k * GT * P, (k + 1) * GT * P)
                for w in ws:
                    dst = (wg, wu, wd)[w]
                    nc.scalar.activation(dst[0][:, c], stage[:, k % 2, w, :], ACT.Copy) \
                        .then_inc(wsplit_hi[k], 1)

            def ffn_chunk(g, first, last, std_n=None):
                for j in range(HT):
                    if std_n == 2 and j in SPLIT_LAST[0]:
                        split_hi(2, (SPLIT_LAST[0].index(j),))
                    if j == XT + 2 and not last:
                        prep_copy(g + 1)
                    if j == CWT + 1 and not last:
                        prep_cwT(g + 1)
                    if j == LOGITS + 1 and not last:
                        prep_sigmoid(g + 1)
                    if std_n == 3 and j == 12:
                        row_std(3)
                    if std_n == 3 and j > MB_SLOT and j - MB_SLOT - 1 < MB:
                        products_hi(j - MB_SLOT - 1)
                    if std_n == 3 and j == HT - 1:
                        a_xT_high(0, psM)
                    act.wait_ge(s["gate_up_ps"], tiles(g, j))
                    if not (first and j < 2):
                        act.wait_ge(s["gated_done"], two_ago(g, j))
                    nc.scalar.activation(silu[j % 2], psG[j % 3][:, :], ACT.Silu) \
                        .then_inc(s["silu_done"], 1)
                    if j == 2 and not first:
                        y_copy(g - 1)
                    if j > 0:
                        z_hi(g, j - 1, first and (j - 1 < 4 or j == HT))
                    elif not first:
                        z_hi(g - 1, HT - 1, False)
                if first:
                    row_std(std_n)

            def ffn(g0):
                ffn_chunk(g0, True, False, 2 if g0 == 0 else 6)
                with act.Fori(g0 + 1, g0 + NC - 1) as g:
                    ffn_chunk(g, False, False)
                ffn_chunk(g0 + NC - 1, False, True, 3 if g0 == 0 else None)
                z_hi(g0 + NC - 1, HT - 1, False)
                if g0 == 0:
                    y_hi(0, 0, True)
                y_copy(g0 + NC - 1)

            def a_xT_high(b, ps):
                act.wait_ge(s["a_xT_ps"], b + 1)
                nc.scalar.activation(key0_of(b), ps[:, 0:P], ACT.Copy).then_inc(s["key0_sb"], 1)
                nc.scalar.activation(of_chunk(xT_parts[0], b), ps[:, :], ACT.Copy) \
                    .then_inc(s["a_xT_hi"], 1)

            def y_hi(b, h, early):
                n = b * H + h
                act.wait_ge(s["yh_ps"], n + 1)
                if not early:
                    act.wait_ge(s["s_ps"], (n - 1) * 3)
                nc.scalar.activation(yh0[:, h % 2, :], psYh[:, 0:P], ACT.Copy) \
                    .then_inc(s["yh_whole"], 1)
                nc.scalar.activation(yh[0][:, h % 2, :], psYh[:, P:], ACT.Copy).then_inc(s["yh_hi"], 1)

            def exp(b, h, qb, early):
                n = b * H + h
                act.wait_ge(s["max_done"], n * TB + (4, 4, 2, 1)[qb])
                if not early:
                    act.wait_ge(s["pT_ps"], (n - 1) * 3)
                o = qb * (qb + 1) // 2 * P
                w = (qb + 1) * P
                nc.scalar.activation(prob[:, h % 2, o:o + w], scores_of(qb), ACT.Exp,
                                     bias=nmax[:, h % 2, qb:qb + 1],
                                     accum_out=rsum[:, h % 2, qb:qb + 1]).then_inc(s["exp_done"], 1)

            def pT_hi(b, h, part, early):
                n = b * H + h
                act.wait_ge(s["pT_ps"], n * 3 + part + 1)
                if not early:
                    act.wait_ge(s["ctx_ps"], n - 1)
                src, o, w = PT_PARTS[part]
                if part == 1:
                    nc.scalar.activation(pT3[:, h % 2, :],
                                         psPT[part][:, 0:P], ACT.Copy).then_inc(s["pT_whole"], 1)
                nc.scalar.activation(pT[0][:, h % 2, o:o + w], psPT[part][:, src:src + w], ACT.Copy) \
                    .then_inc(s["pT_hi"], 1)

            def outT_copy(b):
                act.wait_ge(s["out_ps"], b * H + H)
                nc.scalar.activation(outT, psO[:, :], ACT.Copy).then_inc(s["outT_sb"], 1)

            def ctx_high(b, h, early):
                n = b * H + h
                act.wait_ge(s["ctx_ps"], n + 1)
                if not early:
                    act.wait_ge(s["out_ps"], n - 1)
                nc.scalar.activation(ctx_hi[:, h % 2, :], psC[:, :], ACT.Copy).then_inc(s["ctx_hi"], 1)

            def attn_slot(b, sl, first, last):
                nxt = lambda k: (b, sl + k) if sl + k < H else (b + 1, sl + k - H)
                prv = lambda k: (b, sl - k) if sl >= k else (b - 1, sl - k + H)
                have_y = not (last and sl + 2 >= H)
                have_s = not (last and sl + 1 >= H)
                early = first and sl < 1
                if have_s:
                    exp(*nxt(1), 3, early)
                if have_s:
                    exp(*nxt(1), 2, early)
                pT_hi(b, sl, 0, first and sl < 2)
                if have_s:
                    exp(*nxt(1), 1, early)
                if have_s:
                    exp(*nxt(1), 0, early)
                if have_y:
                    y_hi(*nxt(2), False)
                pT_hi(b, sl, 1, first and sl < 2)
                if not (first and sl < 1):
                    ctx_high(*prv(1), first and sl < 3)
                pT_hi(b, sl, 2, first and sl < 2)
                if sl == 1 and not first:
                    outT_copy(b - 1)
                if sl == 8 and not last:
                    a_xT_high(b + 1, psYh)
                if sl == 8 and last:
                    prep_copy(NC, psYh, xT_first)
                if sl == 9 and last:
                    prep_sigmoid(NC, ps=psYh)
                if sl == 3 and first:
                    row_std(4)
                if sl == 5 and last:
                    row_std(5)

            def products_hi(k):
                act.wait_ge(s["mb_ps"], k + 1)
                src = psM[:, :].rearrange("p (j d) -> p j d", d=P)
                if k < H // TB:
                    nc.scalar.activation(head_columns(mh[0], k), src, ACT.Copy,
                                         scale=float(DK) ** -0.5).then_inc(s["mb_hi"], 1)
                else:
                    nc.scalar.activation(head_columns(b_whole, k), src, ACT.Copy)
                    nc.scalar.activation(head_columns(bh[0], k), src, ACT.Copy) \
                        .then_inc(s["mb_hi"], 1)

            def attention():
                for qb in (3, 2, 1, 0):
                    exp(0, 0, qb, True)
                y_hi(0, 1, True)
                for sl in range(H):
                    attn_slot(0, sl, True, False)
                with act.Fori(1, NC - 1) as b:
                    for sl in range(H):
                        attn_slot(b, sl, False, False)
                for sl in range(H):
                    attn_slot(NC - 1, sl, False, True)
                prep_cwT(NC, psYh)
                ctx_high(NC - 1, H - 1, False)
                outT_copy(NC - 1)

            row_std(0)
            prep_copy(0)
            prep_sigmoid(0, True)
            split_hi(0)
            split_hi(1)
            prep_cwT(0)
            row_std(1)
            ffn(0)
            attention()
            ffn(NC)

        @block.vector
        def _(dve):
            def finish_std(n):
                k = n * 5
                c = slice(STD[n][0] * TB, STD[n][1] * TB)
                dve.wait_ge(s["stat_act"], n + 1)
                nc.vector.reciprocal(rstd0[:, c], std[:, c]).then_inc(s["stat_dve"], 1)
                dve.wait_ge(s["stat_dve"], k + 1)
                nc.vector.tensor_tensor(newton[:, c], rstd0[:, c], rstd0[:, c], ALU.mult) \
                    .then_inc(s["stat_dve"], 1)
                dve.wait_ge(s["stat_dve"], k + 2)
                nc.vector.tensor_tensor(newton[:, c], newton[:, c], var_eps[:, c], ALU.mult) \
                    .then_inc(s["stat_dve"], 1)
                dve.wait_ge(s["stat_dve"], k + 3)
                nc.vector.tensor_scalar(newton[:, c], newton[:, c], -0.5, 1.5, ALU.mult, ALU.add) \
                    .then_inc(s["stat_dve"], 1)
                dve.wait_ge(s["stat_dve"], k + 4)
                nc.vector.tensor_tensor(rstd[:, c], rstd0[:, c], newton[:, c], ALU.mult) \
                    .then_inc(s["stat_dve"], 1)
                dve.wait_ge(s["stat_dve"], k + 5)

            def chunk_stats(c, k):
                rows_stats(c)
                rows_mean(c, k)

            def rows_stats(c):
                nc.vector.tensor_copy(pace[:, :], ident[:, 0:1])
                for t in range(TB):
                    m = nc.vector.bn_stats(bn[:, t, :], x[:, bass.ds(c * TB + t, 1), :]
                                           .rearrange("p a d -> p (a d)"))
                m.then_inc(s["stat_rows"], 1)

            def rows_mean(c, k):
                dve.wait_ge(s["stat_rows"], k * 2 + 1)
                nc.vector.tensor_copy(pace[:, :], ident[:, 0:1])
                for t in range(TB):
                    m = nc.vector.bn_aggr(mean_var[:, t, :], bn[:, t, :])
                m.then_inc(s["stat_rows"], 1)
                dve.wait_ge(s["stat_rows"], k * 2 + 2)
                nc.vector.tensor_copy(mean[:, bass.ds(c * TB, TB)], mean_var[:, :, 0])
                nc.vector.tensor_scalar(var_eps[:, bass.ds(c * TB, TB)], mean_var[:, :, 1],
                                        EPS, None, ALU.add).then_inc(s["stat_bn"], 1)

            def normalise(c, done, ts=range(TB)):
                for t in ts:
                    m = nc.vector.tensor_scalar(
                        xn[:, t, :], x[:, bass.ds(c * TB + t, 1), :].rearrange("p a d -> p (a d)"),
                        mean[:, bass.ds(c * TB + t, 1)], rstd[:, bass.ds(c * TB + t, 1)],
                        ALU.subtract, ALU.mult)
                if t == TB - 1:
                    m.then_inc(s[done], 1)

            def step(ins):
                ins.then_inc(s["route"], 1)

            tt = nc.vector.tensor_tensor

            def route_scores(g):
                dve.wait_ge(s["sigmoid_done"], g + 1)
                step(tt(sc[:, :, :], score[:, :, :], bias[:, :].unsqueeze(1).broadcast_to([P, TB, E]),
                        ALU.add))
                dve.wait_ge(s["route"], g * ROUTE + 1)
                v = sc[:, :, :].rearrange("p t (a b) -> p (t a) b", a=G)
                step(tt(t4[0][:, :, :], v[:, :, 0:4], v[:, :, 4:8], ALU.max))
                step(tt(t4[1][:, :, :], v[:, :, 0:4], v[:, :, 4:8], ALU.min))

            def route_top2(g):
                hi, lo = t4
                dve.wait_ge(s["route"], g * ROUTE + 3)
                step(tt(t2[0][:, :, :], hi[:, :, 0:2], hi[:, :, 2:4], ALU.max))
                step(tt(t2[1][:, :, :], hi[:, :, 0:2], hi[:, :, 2:4], ALU.min))
                step(tt(t2[2][:, :, :], lo[:, :, 0:2], lo[:, :, 2:4], ALU.max))
                dve.wait_ge(s["route"], g * ROUTE + 6)
                step(tt(t2[3][:, :, :], t2[1][:, :, :], t2[2][:, :, :], ALU.max))

            def route_group_score(g):
                hi, lo = t2[0], t2[3]
                dve.wait_ge(s["route"], g * ROUTE + 7)
                step(tt(t1[0][:, :, :], hi[:, :, 0:1], hi[:, :, 1:2], ALU.max))
                step(tt(t1[1][:, :, :], hi[:, :, 0:1], hi[:, :, 1:2], ALU.min))
                step(tt(t1[2][:, :, :], lo[:, :, 0:1], lo[:, :, 1:2], ALU.max))
                dve.wait_ge(s["route"], g * ROUTE + 10)
                step(tt(t1[3][:, :, :], t1[1][:, :, :], t1[2][:, :, :], ALU.max))
                dve.wait_ge(s["route"], g * ROUTE + 11)
                step(tt(gscore[:, :, :], t1[0][:, :, :], t1[3][:, :, :], ALU.add))

            def route_group_rank(g):
                v = gscore[:, :, :].rearrange("p (t a) o -> p t (a o)", t=TB)
                other = v.unsqueeze(2).broadcast_to([P, TB, G, G])
                own = v.unsqueeze(3).broadcast_to([P, TB, G, G])
                dve.wait_ge(s["route"], g * ROUTE + 12)
                step(tt(gcmp[0][:, :, :, :], other, own, ALU.is_gt))
                step(tt(gcmp[1][:, :, :, :], other, own, ALU.is_equal))
                dve.wait_ge(s["route"], g * ROUTE + 14)
                step(tt(gcmp[2][:, :, :, :], gcmp[1][:, :, :, :], tie, ALU.mult))
                dve.wait_ge(s["route"], g * ROUTE + 15)
                step(tt(gcmp[1][:, :, :, :], gcmp[0][:, :, :, :], gcmp[2][:, :, :, :], ALU.add))

            def route_mask(g):
                dve.wait_ge(s["route"], g * ROUTE + 16)
                step(nc.vector.tensor_reduce(grank[:, :, 0], gcmp[1][:, :, :, :]
                                             .rearrange("p t a b -> p (t a) b"), AX.X, ALU.add))
                dve.wait_ge(s["route"], g * ROUTE + 17)
                step(nc.vector.tensor_scalar(gpen[:, :, :], grank[:, :, :], 1.5, NEG,
                                             ALU.is_gt, ALU.mult))
                dve.wait_ge(s["route"], g * ROUTE + 18)
                step(tt(masked[:, :, :].rearrange("p t (a b) -> p (t a) b", a=G),
                        sc[:, :, :].rearrange("p t (a b) -> p (t a) b", a=G),
                        gpen[:, :, :].broadcast_to([P, TB * G, EG]), ALU.add))

            def route_topk(g):
                dve.wait_ge(s["route"], g * ROUTE + 19)
                nc.vector.tensor_copy(pace[:, :], ident[:, 0:1])
                for t in range(TB):
                    step(nc.vector.max(top[:, t, :], masked[:, t, :]))

            def route_places(g):
                dve.wait_ge(s["route"], g * ROUTE + 23)
                nc.vector.tensor_copy(pace[:, :], ident[:, 0:1])
                for t in range(TB):
                    step(nc.vector.max_index(topi[:, t, :], top[:, t, :], masked[:, t, :]))
                dve.wait_ge(s["route"], g * ROUTE + 27)
                step(nc.vector.tensor_copy(topf[:, :, :], topi[:, :, :]))

            def route_onehot(g):
                dve.wait_ge(s["route"], g * ROUTE + 28)
                step(tt(onehot[:, :, :, :], iota.unsqueeze(1).broadcast_to([P, TB, E, TOPK]),
                        topf[:, :, 0:TOPK].unsqueeze(2).broadcast_to([P, TB, E, TOPK]),
                        ALU.is_equal))

            def route_chosen(g):
                dve.wait_ge(s["route"], g * ROUTE + 29)
                step(nc.vector.tensor_reduce(chosen[:, :, :], onehot[:, :, :, :], AX.X, ALU.add))
                step(tt(anch[:, :, :], onehot[:, :, 0:E:2, 0], onehot[:, :, 1:E:2, 0], ALU.add))

            def route_weights(g):
                if not (isinstance(g, int) and g == 0):
                    dve.wait_ge(s["cwT_ps"], g)
                dve.wait_ge(s["route"], g * ROUTE + 31)
                step(tt(wts[:, :, :], chosen[:, :, :], score[:, :, :], ALU.mult))
                step(nc.vector.tensor_scalar(cw[:, :, E:E + L], anch[:, :, :], 0.05, None, ALU.mult))
                dve.wait_ge(s["route"], g * ROUTE + 33)
                step(nc.vector.tensor_reduce(wsum[:, :, 0], wts[:, :, :], AX.X, ALU.add))
                dve.wait_ge(s["route"], g * ROUTE + 34)
                step(nc.vector.tensor_scalar(wsum_e[:, :, :], wsum[:, :, :], 1e-20, None, ALU.add))

            def route_scale(g):
                dve.wait_ge(s["route"], g * ROUTE + 35)
                step(nc.vector.reciprocal(wrec[:, :, :], wsum_e[:, :, :]))
                dve.wait_ge(s["route"], g * ROUTE + 36)
                step(nc.vector.scalar_tensor_tensor(
                    out=cw[:, :, 0:E], in0=wts[:, :, :], scalar=0.1,
                    in1=wrec[:, :, :].broadcast_to([P, TB, E]), op0=ALU.mult, op1=ALU.mult))

            def route_halves(g):
                route_scores(g)
                route_top2(g)

            ROUTING = {7: route_halves, 8: route_group_score, 10: route_group_rank,
                       11: route_mask, 12: route_topk, 13: route_places, 14: route_onehot,
                       15: route_chosen, 16: route_weights, 17: route_scale}

            def xT_low(g, whole=xT):
                dve.wait_ge(s["xT_hi"], g + 1)
                tt(of_chunk(xT_parts[1], g), whole, f32(of_chunk(xT_parts[0], g)), ALU.subtract) \
                    .then_inc(s["xT_lo"], 1)

            def add_y(g, g0):
                xs = x[:, bass.ds((g - g0) * TB, TB), :]
                dve.wait_ge(s["yT_ps"], g + 1)
                tt(xs, xs, psM[:, :].rearrange("p (t d) -> p t d", t=TB), ALU.add) \
                    .then_inc(s["x_added"], 1)

            def ffn_chunk(g, g0, first, last):
                measure = g0 == 0 and not first
                at_stats, at_mean = (10, 11) if last else (19, 20)
                mb = g0 == 0 and last
                for j in range(HT):
                    if j == 0 and not last:
                        dve.wait_ge(s["xT_ps"], g + 1)
                        normalise(g + 1 - g0, "xn_ready")
                    if mb and j > MB_SLOT and j - MB_SLOT - 1 < H // TB:
                        products_lo(j - MB_SLOT - 1)
                    dve.wait_ge(s["silu_done"], tiles(g, j))
                    if not (first and j < 3):
                        dve.wait_ge(s["z_lo"], tiles(g, j) - 3)
                    tt(z[j % 3], psU[j % 3][:, :], silu[j % 2], ALU.mult).then_inc(s["gated_done"], 1)
                    if j == 9 and not first:
                        add_y(g - 1, g0)
                    if j == XT + 3 and not last:
                        xT_low(g + 1)
                    if j in ROUTING and not last:
                        ROUTING[j](g + 1)
                    if j == at_stats and measure:
                        dve.wait_ge(s["x_added"], g)
                        rows_stats(g - 1)
                    if j == at_mean and measure:
                        rows_mean(g - 1, g - 1 + NC)
                    if first and g0 == 0 and j in FIRST_STATS:
                        c = FIRST_STATS[j]
                        dve.wait_ge(x_loads[c], 16)
                        chunk_stats(c, c)
                    if mb and j == 15:
                        finish_std(3)
                    if mb and j == 16:
                        a_rows(0, True, range(TB))
                    if mb and j == 17:
                        a_residual(0)
                    dve.wait_ge(s["gated_done"], tiles(g, j))
                    if j < SPREAD_TILES:
                        dve.wait_ge(spread_loads[j % NSPREAD], spread_count(g, j))
                        tt(z[j % 3], z[j % 3], spread[:, j % NSPREAD, :], ALU.mult) \
                            .then_inc(s["z_done"], 1)
                    else:
                        nc.vector.tensor_scalar(z[j % 3], z[j % 3], 0.5, None, ALU.mult) \
                            .then_inc(s["z_done"], 1)
                if mb:
                    a_xT_low(0, psM)
                if first:
                    finish_std(2 if g0 == 0 else 6)

            def ffn(g0):
                ffn_chunk(g0, g0, True, False)
                with dve.Fori(g0 + 1, g0 + NC - 1) as g:
                    ffn_chunk(g, g0, False, False)
                ffn_chunk(g0 + NC - 1, g0, False, True)

            FIRST_STATS = dict(zip((2, 3, 4, 6, 9, 19), range(2, NC)))

            def products_lo(k):
                dve.wait_ge(s["mb_hi"], k + 1)
                nc.vector.scalar_tensor_tensor(
                    out=head_columns(mh[1], k), in0=psM[:, :].rearrange("p (j d) -> p j d", d=P),
                    scalar=float(DK) ** -0.5, in1=f32(head_columns(mh[0], k)),
                    op0=ALU.mult, op1=ALU.subtract).then_inc(s["mb_lo"], 1)

            def a_rows(b, first, ts):
                if not first and ts[0] == 0:
                    dve.wait_ge(s["a_xT_ps"], b)
                    dve.wait_ge(s["a_xn_lo"], b)
                normalise(b, "a_xn", ts)

            def a_residual(b):
                dve.wait_ge(s["a_xn"], b + 1)
                xs = x[:, bass.ds(b * TB, TB), :]
                tt(xs, xs, xn[:, :, :], ALU.add).then_inc(s["a_xres"], 1)

            def a_xT_low(b, ps):
                dve.wait_ge(s["a_xT_hi"], b + 1)
                tt(of_chunk(xT_parts[1], b), ps[:, :], f32(of_chunk(xT_parts[0], b)), ALU.subtract) \
                    .then_inc(s["a_xT_lo"], 1)

            def a_row_parts(b, first):
                if not first:
                    dve.wait_ge(s["ctx_ps"], b * H)
                nc.vector.tensor_copy(rows3, xn[:, TB - 1, :]).then_inc(s["rows3_sb"], 1)
                nc.vector.tensor_copy(xnp[0][:, :, :], xn[:, :, :]).then_inc(s["a_xn_hi"], 1)
                dve.wait_ge(s["a_xn_hi"], b + 1)
                tt(xnp[1][:, :, :], xn[:, :, :], f32(xnp[0][:, :, :]), ALU.subtract) \
                    .then_inc(s["a_xn_lo"], 1)

            def y_lo(b, h):
                n = b * H + h
                dve.wait_ge(s["yh_hi"], n + 1)
                tt(yh[1][:, h % 2, :], psYh[:, P:], f32(yh[0][:, h % 2, :]), ALU.subtract) \
                    .then_inc(s["yh_lo"], 1)

            def row_max(b, h, qb):
                n = b * H + h
                dve.wait_ge(s["s_ps"], n * 3 + (3, 3, 2, 1)[qb])
                nc.vector.tensor_reduce(nmax[:, h % 2, qb:qb + 1], scores_of(qb),
                                        AX.X, ALU.max, negate=True).then_inc(s["max_done"], 1)

            def pT_lo(b, h, part):
                n = b * H + h
                dve.wait_ge(s["pT_hi"], n * 3 + part + 1)
                src, o, w = PT_PARTS[part]
                tt(pT[1][:, h % 2, o:o + w], psPT[part][:, src:src + w], f32(pT[0][:, h % 2, o:o + w]),
                   ALU.subtract).then_inc(s["pT_lo"], 1)

            def row_rec(b, h, qb):
                n = b * H + h
                dve.wait_ge(s["exp_done"], n * TB + TB - qb)
                nc.vector.reciprocal(rrec[:, h % 2, qb:qb + 1], rsum[:, h % 2, qb:qb + 1]) \
                    .then_inc(s["rec_done"], 1)

            def b_low(i):
                c = slice(i * TB * P, (i + 1) * TB * P)
                dve.wait_ge(s["mb_hi"], MB)
                tt(bh[1][:, c], b_whole[:, c], f32(bh[0][:, c]), ALU.subtract).then_inc(s["b_lo"], 1)

            def ctx_low(b, h, early):
                n = b * H + h
                dve.wait_ge(s["ctx_hi"], n + 1)
                if not early:
                    dve.wait_ge(s["out_ps"], n)
                tt(ctx_lo[:, :], psC[:, :], f32(ctx_hi[:, h % 2, :]), ALU.subtract) \
                    .then_inc(s["ctx_lo"], 1)

            def add_out(b):
                dve.wait_ge(s["outT_ps"], b + 1)
                dve.wait_ge(s["a_xres"], b + 1)
                xs = x[:, bass.ds(b * TB, TB), :]
                tt(xs, xs, psO[:, :].rearrange("p (t d) -> p t d", t=TB), ALU.add) \
                    .then_inc(s["out_added"], 1)

            def attn_slot(b, sl, first, last):
                nxt = lambda k: (b, sl + k) if sl + k < H else (b + 1, sl + k - H)
                prv = lambda k: (b, sl - k) if sl >= k else (b - 1, sl - k + H)
                have_y = not (last and sl + 2 >= H)
                have_s = not (last and sl + 1 >= H)
                if not (first and sl < 1):
                    pT_lo(*prv(1), 2)
                if have_s:
                    row_max(*nxt(1), 3)
                if have_s:
                    row_max(*nxt(1), 2)
                if sl == 9 and not last:
                    a_xT_low(b + 1, psYh)
                if sl == 9 and last:
                    xT_low(NC, xT_first)
                if have_s:
                    row_max(*nxt(1), 1)
                if have_s:
                    row_max(*nxt(1), 0)
                if not (first and sl < 2):
                    ctx_low(*prv(2), first and sl < 3)
                if have_s:
                    row_rec(*nxt(1), 3)
                if have_s:
                    row_rec(*nxt(1), 2)
                pT_lo(b, sl, 0)
                if have_s:
                    row_rec(*nxt(1), 1)
                if have_s:
                    row_rec(*nxt(1), 0)
                if sl == 2 and not first:
                    add_out(b - 1)
                if have_y:
                    y_lo(*nxt(2))
                pT_lo(b, sl, 1)
                if sl < 2 and first:
                    b_low(2 * sl)
                    b_low(2 * sl + 1)
                if sl == 0:
                    a_row_parts(b, first)
                if sl == 1 and first:
                    dve.wait_ge(s["x_added"], NC)
                    chunk_stats(NC - 1, 2 * NC - 1)
                if sl == 3 and not first:
                    dve.wait_ge(s["out_added"], b)
                    rows_stats(b - 1)
                if sl == 4 and not first:
                    rows_mean(b - 1, b - 1 + 2 * NC)
                if sl in (5, 6) and not last:
                    a_rows(b + 1, False, (2 * (sl - 5), 2 * (sl - 5) + 1))
                if sl == 7 and not last:
                    a_residual(b + 1)
                if sl == 4 and first:
                    finish_std(4)
                if sl == 6 and last:
                    finish_std(5)
                if sl == 7 and last:
                    normalise(0, "xn_ready")
                if last and sl == H - 1:
                    pT_lo(b, sl, 2)
                if last and sl >= 10:
                    for k in list(ROUTING)[2 * (sl - 10):2 * (sl - 9)]:
                        ROUTING[k](NC)

            def attention():
                y_lo(0, 0)
                for qb in (3, 2, 1, 0):
                    row_max(0, 0, qb)
                for qb in (3, 2, 1, 0):
                    row_rec(0, 0, qb)
                y_lo(0, 1)
                add_y(NC - 1, 0)
                for sl in range(H):
                    attn_slot(0, sl, True, False)
                with dve.Fori(1, NC - 1) as b:
                    for sl in range(H):
                        attn_slot(b, sl, False, False)
                for sl in range(H):
                    attn_slot(NC - 1, sl, False, True)
                ctx_low(NC - 1, H - 2, False)
                ctx_low(NC - 1, H - 1, False)
                add_out(NC - 1)
                dve.wait_ge(s["out_added"], NC)
                chunk_stats(NC - 1, 3 * NC - 1)

            dve.wait_ge(s["consts_loaded"], 48)
            dve.wait_ge(x_loads[0], 16)
            chunk_stats(0, 0)
            finish_std(0)
            normalise(0, "xn_ready")
            nc.vector.tensor_copy(half[:, 0:2 * P], small[:, 0:2 * P])
            nc.vector.tensor_copy(half[:, 2 * P:], small[:, P:2 * P])
            nc.vector.memset(cw[:, :, ROWS:], 0.0)
            xT_low(0)
            for k in ROUTING:
                ROUTING[k](0)
            dve.wait_ge(x_loads[1], 16)
            chunk_stats(1, 1)
            finish_std(1)
            ffn(0)
            attention()
            ffn(NC)
            add_y(2 * NC - 1, NC)

        @block.gpsimd
        def _(pool):
            def split_lo(k, w):
                c = slice(k * GT * P, (k + 1) * GT * P)
                dst = (wg, wu, wd)[w]
                pool.wait_ge(wsplit_hi[k], w + 1)
                nc.gpsimd.tensor_tensor(dst[1][:, c], stage[:, k % 2, w, :], f32(dst[0][:, c]),
                                        ALU.subtract).then_inc(wsplit[k], 1)

            for w in range(3):
                split_lo(0, w)
            for w in range(3):
                split_lo(1, w)
            pool.wait_ge(s["consts_loaded"], 48)

            def z_low(g, j):
                pool.wait_ge(s["z_hi"], tiles(g, j))
                nc.gpsimd.tensor_tensor(zp[1][part_slot(j)], z[j % 3], f32(zp[0][part_slot(j)]),
                                        ALU.subtract).then_inc(s["z_lo"], 1)

            def norm(n, par):
                for qb in (3, 2, 1, 0):
                    pool.wait_ge(s["rec_done"], (2 * n + par) * TB + TB - qb)
                    k = par * TB + qb
                    nc.gpsimd.tensor_tensor(pool_pace[:, k:k + 1], ident[:, 0:1], ident[:, 0:1], ALU.add)
                    o = qb * (qb + 1) // 2 * P
                    p = prob[:, par, o:o + (qb + 1) * P]
                    nc.gpsimd.tensor_scalar(p, p, rrec[:, par, qb:qb + 1], 1.0, ALU.mult, ALU.mult) \
                        .then_inc(s["norm_done"], 1)

            for j in range(HT):
                if j in SPLIT_LAST[1]:
                    split_lo(2, SPLIT_LAST[1].index(j))
                z_low(0, j)
            with pool.Fori(1, NC) as g:
                for j in range(HT):
                    z_low(g, j)
            with pool.Fori(0, NC * H // 2) as n:
                norm(n, 0)
                norm(n, 1)
            with pool.Fori(NC, 2 * NC) as g:
                for j in range(HT):
                    z_low(g, j)


def kernel(L0_attn_x, L0_attn_Wq, L0_attn_Wk, L0_attn_Wv, L0_attn_Wo, L0_ffn_gate_weight,
           L0_ffn_gate_bias, L0_ffn_w_gate, L0_ffn_w_up, L0_ffn_w_down, L0_ffn_shared_w_gate,
           L0_ffn_shared_w_up, L0_ffn_shared_w_down, L0_ffn_anchor_w_gate, L0_ffn_anchor_w_up,
           L0_ffn_anchor_w_down):
    import concourse.bacc as bacc
    from concourse.bass_utils import run_bass_kernel_spmd

    x = np.asarray(L0_attn_x)
    B, S, D = x.shape

    def hidden_columns(experts, anchors, shared):
        parts = [np.asarray(w).transpose(1, 0, 2).reshape(D, -1) for w in (experts, anchors)]
        parts.append(np.asarray(shared))
        w = np.zeros((D, HT * P), np.float32)
        w[:, :sum(p.shape[1] for p in parts)] = np.concatenate(parts, 1)
        return w

    down = np.zeros((HT * P, D), np.float32)
    rows = np.concatenate([np.asarray(L0_ffn_w_down).reshape(-1, D),
                           np.asarray(L0_ffn_anchor_w_down).reshape(-1, D),
                           np.asarray(L0_ffn_shared_w_down)], 0)
    down[:rows.shape[0]] = rows
    arrays = {
        "x": x.reshape(B * S, D),
        "w_gate": hidden_columns(L0_ffn_w_gate, L0_ffn_anchor_w_gate, L0_ffn_shared_w_gate),
        "w_up": hidden_columns(L0_ffn_w_up, L0_ffn_anchor_w_up, L0_ffn_shared_w_up),
        "w_down": down.reshape(HT, P, D).transpose(1, 0, 2).reshape(P, HT * D),
        "gate_weight": np.asarray(L0_ffn_gate_weight).T,
        "gate_bias": np.asarray(L0_ffn_gate_bias),
        "wqT": np.asarray(L0_attn_Wq).T,
        "wkT": np.asarray(L0_attn_Wk).T,
        "wvT": np.asarray(L0_attn_Wv).T,
        "wo": np.asarray(L0_attn_Wo),
        "small": constants(),
    }
    arrays = {n: np.ascontiguousarray(a) for n, a in arrays.items()}
    nc = bacc.Bacc("TRN2", target_bir_lowering=False, num_devices=1)
    args = [nc.dram_tensor("in_" + n, a.shape, mybir.dt.from_np(a.dtype), kind="ExternalInput").ap()
            for n, a in arrays.items()]
    out = nc.dram_tensor("out_rows", (B * S, D), F32, kind="ExternalOutput").ap()
    cw_rows = nc.dram_tensor("cw_rows", (2 * ROWS, CH), F32).ap()
    build(nc, *args, cw_rows, out)
    r = run_bass_kernel_spmd(nc, [{"in_" + n: a for n, a in arrays.items()}], core_ids=[0])
    return r.results[0]["out_rows"].reshape(B, S, D)
```
